# Optimizing a Trainium2 kernel written in Bass

```python
import numpy as np
import jax
import jax.numpy as jnp

def _softmax(x, axis=-1):
    return jax.nn.softmax(x, axis=axis)

def _gelu(x):
    return jax.nn.gelu(x, approximate=True)

def _silu(x):
    return jax.nn.silu(x)

def _sigmoid(x):
    return jax.nn.sigmoid(x)

def _layernorm(x, axis=-1, eps=1e-05):
    m = jnp.mean(x, axis=axis, keepdims=True)
    v = jnp.var(x, axis=axis, keepdims=True)
    return (x - m) / jnp.sqrt(v + eps)

def _scatter_add(tgt, idx, src, axis=0):
    return tgt.at[idx].add(src)

def _segment_sum(src, seg, n):
    return jax.ops.segment_sum(src, seg, n)
kernel_name = 'mk_dlrm_tower_d1_rec_r8_0c4159'

def setup_inputs(seed: int=0):
    np.random.seed(seed)
    _w = jnp.asarray

    def _rec_inputs():
        import jax
        import jax.numpy as jnp
        _tk = jax.random.key(seed)
        dense_ctx = jax.random.normal(jax.random.fold_in(_tk, 190), (2048, 16), jnp.float32)
        ids = jnp.stack([jax.random.randint(jax.random.fold_in(_tk, 200 + f), (2048,), 0, v, jnp.int32) for f, v in enumerate([12500, 1000, 12500, 1000, 1000, 1250, 1000, 1000, 1250, 1000, 1250, 125000, 1000, 125000, 12500, 125000, 12500, 125000, 12500, 12500, 12500, 1000, 125000, 12500, 1250, 12500, 1000, 125000, 125000, 1000, 1000, 125000, 1000, 125000, 1000, 1250, 12500, 12500, 1000])], axis=1)
        tbl_0 = 0.05 * jax.random.normal(jax.random.fold_in(_tk, 500 + 0), (12500, 16), jnp.float32)
        tbl_1 = 0.05 * jax.random.normal(jax.random.fold_in(_tk, 500 + 1), (1000, 16), jnp.float32)
        tbl_2 = 0.05 * jax.random.normal(jax.random.fold_in(_tk, 500 + 2), (12500, 16), jnp.float32)
        tbl_3 = 0.05 * jax.random.normal(jax.random.fold_in(_tk, 500 + 3), (1000, 16), jnp.float32)
        tbl_4 = 0.05 * jax.random.normal(jax.random.fold_in(_tk, 500 + 4), (1000, 16), jnp.float32)
        tbl_5 = 0.05 * jax.random.normal(jax.random.fold_in(_tk, 500 + 5), (1250, 16), jnp.float32)
        tbl_6 = 0.05 * jax.random.normal(jax.random.fold_in(_tk, 500 + 6), (1000, 16), jnp.float32)
        tbl_7 = 0.05 * jax.random.normal(jax.random.fold_in(_tk, 500 + 7), (1000, 16), jnp.float32)
        tbl_8 = 0.05 * jax.random.normal(jax.random.fold_in(_tk, 500 + 8), (1250, 16), jnp.float32)
        tbl_9 = 0.05 * jax.random.normal(jax.random.fold_in(_tk, 500 + 9), (1000, 16), jnp.float32)
        tbl_10 = 0.05 * jax.random.normal(jax.random.fold_in(_tk, 500 + 10), (1250, 16), jnp.float32)
        tbl_11 = 0.05 * jax.random.normal(jax.random.fold_in(_tk, 500 + 11), (125000, 16), jnp.float32)
        tbl_12 = 0.05 * jax.random.normal(jax.random.fold_in(_tk, 500 + 12), (1000, 16), jnp.float32)
        tbl_13 = 0.05 * jax.random.normal(jax.random.fold_in(_tk, 500 + 13), (125000, 16), jnp.float32)
        tbl_14 = 0.05 * jax.random.normal(jax.random.fold_in(_tk, 500 + 14), (12500, 16), jnp.float32)
        tbl_15 = 0.05 * jax.random.normal(jax.random.fold_in(_tk, 500 + 15), (125000, 16), jnp.float32)
        tbl_16 = 0.05 * jax.random.normal(jax.random.fold_in(_tk, 500 + 16), (12500, 16), jnp.float32)
        tbl_17 = 0.05 * jax.random.normal(jax.random.fold_in(_tk, 500 + 17), (125000, 16), jnp.float32)
        tbl_18 = 0.05 * jax.random.normal(jax.random.fold_in(_tk, 500 + 18), (12500, 16), jnp.float32)
        tbl_19 = 0.05 * jax.random.normal(jax.random.fold_in(_tk, 500 + 19), (12500, 16), jnp.float32)
        tbl_20 = 0.05 * jax.random.normal(jax.random.fold_in(_tk, 500 + 20), (12500, 16), jnp.float32)
        tbl_21 = 0.05 * jax.random.normal(jax.random.fold_in(_tk, 500 + 21), (1000, 16), jnp.float32)
        tbl_22 = 0.05 * jax.random.normal(jax.random.fold_in(_tk, 500 + 22), (125000, 16), jnp.float32)
        tbl_23 = 0.05 * jax.random.normal(jax.random.fold_in(_tk, 500 + 23), (12500, 16), jnp.float32)
        tbl_24 = 0.05 * jax.random.normal(jax.random.fold_in(_tk, 500 + 24), (1250, 16), jnp.float32)
        tbl_25 = 0.05 * jax.random.normal(jax.random.fold_in(_tk, 500 + 25), (12500, 16), jnp.float32)
        tbl_26 = 0.05 * jax.random.normal(jax.random.fold_in(_tk, 500 + 26), (1000, 16), jnp.float32)
        tbl_27 = 0.05 * jax.random.normal(jax.random.fold_in(_tk, 500 + 27), (125000, 16), jnp.float32)
        tbl_28 = 0.05 * jax.random.normal(jax.random.fold_in(_tk, 500 + 28), (125000, 16), jnp.float32)
        tbl_29 = 0.05 * jax.random.normal(jax.random.fold_in(_tk, 500 + 29), (1000, 16), jnp.float32)
        tbl_30 = 0.05 * jax.random.normal(jax.random.fold_in(_tk, 500 + 30), (1000, 16), jnp.float32)
        tbl_31 = 0.05 * jax.random.normal(jax.random.fold_in(_tk, 500 + 31), (125000, 16), jnp.float32)
        tbl_32 = 0.05 * jax.random.normal(jax.random.fold_in(_tk, 500 + 32), (1000, 16), jnp.float32)
        tbl_33 = 0.05 * jax.random.normal(jax.random.fold_in(_tk, 500 + 33), (125000, 16), jnp.float32)
        tbl_34 = 0.05 * jax.random.normal(jax.random.fold_in(_tk, 500 + 34), (1000, 16), jnp.float32)
        tbl_35 = 0.05 * jax.random.normal(jax.random.fold_in(_tk, 500 + 35), (1250, 16), jnp.float32)
        tbl_36 = 0.05 * jax.random.normal(jax.random.fold_in(_tk, 500 + 36), (12500, 16), jnp.float32)
        tbl_37 = 0.05 * jax.random.normal(jax.random.fold_in(_tk, 500 + 37), (12500, 16), jnp.float32)
        tbl_38 = 0.05 * jax.random.normal(jax.random.fold_in(_tk, 500 + 38), (1000, 16), jnp.float32)
        _rk = jax.random.fold_in(_tk, 7)
        W_top1 = 0.0606339 * jax.random.normal(jax.random.fold_in(_tk, 801), (272, 512), jnp.float32)
        W_top2 = 0.0441942 * jax.random.normal(jax.random.fold_in(_tk, 802), (512, 256), jnp.float32)
        W_top3 = 0.0625 * jax.random.normal(jax.random.fold_in(_tk, 803), (256, 1), jnp.float32)
        b_top1 = jnp.zeros((512,), jnp.float32)
        b_top2 = jnp.zeros((256,), jnp.float32)
        return (dense_ctx, ids, tbl_0, tbl_1, tbl_2, tbl_3, tbl_4, tbl_5, tbl_6, tbl_7, tbl_8, tbl_9, tbl_10, tbl_11, tbl_12, tbl_13, tbl_14, tbl_15, tbl_16, tbl_17, tbl_18, tbl_19, tbl_20, tbl_21, tbl_22, tbl_23, tbl_24, tbl_25, tbl_26, tbl_27, tbl_28, tbl_29, tbl_30, tbl_31, tbl_32, tbl_33, tbl_34, tbl_35, tbl_36, tbl_37, tbl_38, W_top1, b_top1, W_top2, b_top2, W_top3)
    dense_ctx, ids, tbl_0, tbl_1, tbl_2, tbl_3, tbl_4, tbl_5, tbl_6, tbl_7, tbl_8, tbl_9, tbl_10, tbl_11, tbl_12, tbl_13, tbl_14, tbl_15, tbl_16, tbl_17, tbl_18, tbl_19, tbl_20, tbl_21, tbl_22, tbl_23, tbl_24, tbl_25, tbl_26, tbl_27, tbl_28, tbl_29, tbl_30, tbl_31, tbl_32, tbl_33, tbl_34, tbl_35, tbl_36, tbl_37, tbl_38, W_top1, b_top1, W_top2, b_top2, W_top3 = _rec_inputs()

    def _L0_rec_setup():
        import jax, jax.numpy as jnp
        import numpy as np
        NUM_FIELD = 39
        CIN_SIZE = [128, 128]
        EMBED_DIM = 16
        BATCH = 256
        key = jax.random.key(seed)
        k1, k2, k3 = jax.random.split(key, 3)
        x_emb = jax.random.normal(k1, (BATCH, NUM_FIELD, EMBED_DIM), dtype=jnp.float32)
        W0 = jax.random.normal(k2, (CIN_SIZE[0], NUM_FIELD * NUM_FIELD), dtype=jnp.float32) * 0.02
        W1 = jax.random.normal(k3, (CIN_SIZE[1], CIN_SIZE[0] * NUM_FIELD), dtype=jnp.float32) * 0.02
        return {'x_emb': x_emb, 'W0': W0, 'W1': W1}
    _L0_rec_all = _L0_rec_setup()
    _L0_rec_in = {k: v for k, v in _L0_rec_all.items() if k in ('W0', 'W1')}
    del _L0_rec_all
    return {'dense_ctx': dense_ctx, 'ids': ids, 'tbl_0': tbl_0, 'tbl_1': tbl_1, 'tbl_2': tbl_2, 'tbl_3': tbl_3, 'tbl_4': tbl_4, 'tbl_5': tbl_5, 'tbl_6': tbl_6, 'tbl_7': tbl_7, 'tbl_8': tbl_8, 'tbl_9': tbl_9, 'tbl_10': tbl_10, 'tbl_11': tbl_11, 'tbl_12': tbl_12, 'tbl_13': tbl_13, 'tbl_14': tbl_14, 'tbl_15': tbl_15, 'tbl_16': tbl_16, 'tbl_17': tbl_17, 'tbl_18': tbl_18, 'tbl_19': tbl_19, 'tbl_20': tbl_20, 'tbl_21': tbl_21, 'tbl_22': tbl_22, 'tbl_23': tbl_23, 'tbl_24': tbl_24, 'tbl_25': tbl_25, 'tbl_26': tbl_26, 'tbl_27': tbl_27, 'tbl_28': tbl_28, 'tbl_29': tbl_29, 'tbl_30': tbl_30, 'tbl_31': tbl_31, 'tbl_32': tbl_32, 'tbl_33': tbl_33, 'tbl_34': tbl_34, 'tbl_35': tbl_35, 'tbl_36': tbl_36, 'tbl_37': tbl_37, 'tbl_38': tbl_38, 'W_top1': W_top1, 'b_top1': b_top1, 'W_top2': W_top2, 'b_top2': b_top2, 'W_top3': W_top3, 'L0_rec_W0': _L0_rec_in['W0'], 'L0_rec_W1': _L0_rec_in['W1']}

def reference(dense_ctx, ids, tbl_0, tbl_1, tbl_2, tbl_3, tbl_4, tbl_5, tbl_6, tbl_7, tbl_8, tbl_9, tbl_10, tbl_11, tbl_12, tbl_13, tbl_14, tbl_15, tbl_16, tbl_17, tbl_18, tbl_19, tbl_20, tbl_21, tbl_22, tbl_23, tbl_24, tbl_25, tbl_26, tbl_27, tbl_28, tbl_29, tbl_30, tbl_31, tbl_32, tbl_33, tbl_34, tbl_35, tbl_36, tbl_37, tbl_38, W_top1, b_top1, W_top2, b_top2, W_top3, L0_rec_W0, L0_rec_W1):
    import jax
    import jax.numpy as jnp

    def _L0_rec_ref(x_emb, W0, W1):
        import jax, jax.numpy as jnp
        import numpy as np
        NUM_FIELD = 39
        CIN_SIZE = [128, 128]
        EMBED_DIM = 16
        BATCH = 256
        B, F, D = x_emb.shape
        x = x_emb
        outs = []
        for W in (W0, W1):
            last = x.shape[1]
            inter = (x[:, :, None, :] * x_emb[:, None, :, :]).reshape(B, last * F, D)
            x = jnp.einsum('bid,hi->bhd', inter, W)
            outs.append(x.sum(axis=-1))
        return jnp.concatenate(outs, axis=-1)
    e = jnp.stack([tbl_0[ids[:, 0]], tbl_1[ids[:, 1]], tbl_2[ids[:, 2]], tbl_3[ids[:, 3]], tbl_4[ids[:, 4]], tbl_5[ids[:, 5]], tbl_6[ids[:, 6]], tbl_7[ids[:, 7]], tbl_8[ids[:, 8]], tbl_9[ids[:, 9]], tbl_10[ids[:, 10]], tbl_11[ids[:, 11]], tbl_12[ids[:, 12]], tbl_13[ids[:, 13]], tbl_14[ids[:, 14]], tbl_15[ids[:, 15]], tbl_16[ids[:, 16]], tbl_17[ids[:, 17]], tbl_18[ids[:, 18]], tbl_19[ids[:, 19]], tbl_20[ids[:, 20]], tbl_21[ids[:, 21]], tbl_22[ids[:, 22]], tbl_23[ids[:, 23]], tbl_24[ids[:, 24]], tbl_25[ids[:, 25]], tbl_26[ids[:, 26]], tbl_27[ids[:, 27]], tbl_28[ids[:, 28]], tbl_29[ids[:, 29]], tbl_30[ids[:, 30]], tbl_31[ids[:, 31]], tbl_32[ids[:, 32]], tbl_33[ids[:, 33]], tbl_34[ids[:, 34]], tbl_35[ids[:, 35]], tbl_36[ids[:, 36]], tbl_37[ids[:, 37]], tbl_38[ids[:, 38]]], axis=1)
    z = _L0_rec_ref(e, L0_rec_W0, L0_rec_W1)
    z = z.reshape(z.shape[0], -1)
    h = jnp.concatenate([z, dense_ctx], axis=1)
    h = jnp.maximum(h @ W_top1 + b_top1, 0.0)
    h = jnp.maximum(h @ W_top2 + b_top2, 0.0)
    y = h @ W_top3
    return y

_drawn_inputs = setup_inputs


def setup_inputs(seed=0):
    import zlib

    import numpy as np

    out = dict(_drawn_inputs(seed))
    spreads = {'b_top1': (0.0, 0.1), 'b_top2': (0.0, 0.1)}
    factors = {'tbl_0': 8.0,
     'tbl_1': 8.0,
     'tbl_2': 8.0,
     'tbl_3': 8.0,
     'tbl_4': 8.0,
     'tbl_5': 8.0,
     'tbl_6': 8.0,
     'tbl_7': 8.0,
     'tbl_8': 8.0,
     'tbl_9': 8.0,
     'tbl_10': 8.0,
     'tbl_11': 8.0,
     'tbl_12': 8.0,
     'tbl_13': 8.0,
     'tbl_14': 8.0,
     'tbl_15': 8.0,
     'tbl_16': 8.0,
     'tbl_17': 8.0,
     'tbl_18': 8.0,
     'tbl_19': 8.0,
     'tbl_20': 8.0,
     'tbl_21': 8.0,
     'tbl_22': 8.0,
     'tbl_23': 8.0,
     'tbl_24': 8.0,
     'tbl_25': 8.0,
     'tbl_26': 8.0,
     'tbl_27': 8.0,
     'tbl_28': 8.0,
     'tbl_29': 8.0,
     'tbl_30': 8.0,
     'tbl_31': 8.0,
     'tbl_32': 8.0,
     'tbl_33': 8.0,
     'tbl_34': 8.0,
     'tbl_35': 8.0,
     'tbl_36': 8.0,
     'tbl_37': 8.0,
     'tbl_38': 8.0,
     'L0_rec_W1': 8.0}
    for name, (base, spread) in spreads.items():
        noise = np.random.default_rng([zlib.crc32(name.encode()), seed]).standard_normal(out[name].shape)
        drawn = base * np.exp(spread * noise) if base else spread * noise
        out[name] = jnp.asarray(drawn.astype(out[name].dtype))
    for name, factor in factors.items():
        out[name] = (out[name] * factor).astype(out[name].dtype)
    return out
```

```python
from contextlib import ExitStack

import concourse.bass as bass
from concourse import mybir

ALU = mybir.AluOpType
ACT = mybir.ActivationFunctionType
F32 = mybir.dt.float32
F32R = mybir.dt.float32r
BF16 = mybir.dt.bfloat16
I32 = mybir.dt.int32

B, F, D, H = 2048, 39, 16, 128
K0, N1, N2 = 16, 512, 256
P = 128
TB = P
TILES = B // TB
COLS = 512
BB = COLS // D
BLOCKS = TB // BB
GB = P // D
GROUPS = BB // GB
SHIFTS = (F + 1) // 2
R = 3
KP = R * F
CH = -(-SHIFTS // R)
ENTRIES = (CH + 1) // 2
J = F + 1
TABLES = [f"tbl_{f}" for f in range(F)]
SLOTS = 2 * BLOCKS
PAIR = 2
S_IT = PAIR * SLOTS
TAIL = 12
ITERS = TILES // PAIR
OUT1_STEPS = 5
OUT1_J = 8
assert ENTRIES == 4 and CH * R >= SHIFTS and F % 2 == 1


def count(it, per, local):
    return it * per + local


def wait(eng, sem, value):
    if not isinstance(value, int) or value > 0:
        eng.wait_ge(sem, value)


def slots(eng, emit):
    for q in range(S_IT):
        emit(0, q)
    with eng.Fori(1, ITERS - 1, 1) as it:
        for q in range(S_IT):
            emit(it, q)
    for it in (ITERS - 1, ITERS):
        for q in range(S_IT if it < ITERS else TAIL):
            emit(it, q)


def stage(it, q, lag, every=2):
    local = (q - lag) // every
    if isinstance(it, int):
        n = it * (S_IT // every) + local
        return 0 <= n < TILES * SLOTS // every, local
    return True, local


def build(nc, dense_ctx, ids, tables, W_top1, b_top1, W_top2, b_top2, W_top3, W0, W1, out):
    with ExitStack() as ctx:
        def sb(name, shape, dt=F32):
            return ctx.enter_context(nc.sbuf_tensor(name, shape, dt))

        def ps(name, shape):
            return ctx.enter_context(nc.psum_tensor(name, shape, F32))

        def sem(name):
            return ctx.enter_context(nc.semaphore(name))

        idx = sb("idx", [P, 2, F], I32)
        emb = sb("emb", [P, 2, F, D])
        rest = sb("rest", [P, F, D])
        parts = sb("parts", [P, D, 3, F], BF16)
        embT = sb("embT", [P, 2, TB, D], BF16)
        opA = sb("opA", [P, 2, COLS])
        hi = sb("hi", [P, ENTRIES, 2, COLS], F32R)
        lo = sb("lo", [P, ENTRIES, 2, COLS], F32R)
        x1 = sb("x1", [P, 2, COLS])
        xTh = sb("xTh", [P, GROUPS, H], F32R)
        xTl = sb("xTl", [P, GROUPS, H], F32R)
        erow = sb("erow", [P, GROUPS, 2, J], F32R)
        diag = sb("diag", [P, GROUPS, GB, 2, J], F32R)
        gram = sb("gram", [P, 2, J, TB])
        w0h = sb("w0h", [P, CH, H], F32R)
        w0l = sb("w0l", [P, CH, H], F32R)
        w1T = sb("w1T", [P, F, H])
        wt1 = sb("wt1", [P, 2, N1])
        wt1d = sb("wt1d", [K0, N1])
        wt2 = sb("wt2", [P, N1 // P, N2])
        wt3 = sb("wt3", [P, N2 // P])
        bt1 = sb("bt1", [P, N1 // P])
        bt2 = sb("bt2", [P, N2 // P])
        pairs = sb("pairs", [P, CH * R, F])
        dense = sb("dense", [P, TILES, K0])
        denseT = sb("denseT", [K0, B])
        z1 = sb("z1", [P, TB])
        h1 = sb("h1", [P, N1 // P, TB])
        h2 = sb("h2", [P, N2 // P, TB])
        y = sb("y", [1, 2, TB])
        id32 = sb("id32", [P, P])
        id16 = sb("id16", [P, P], BF16)
        match = sb("match", [KP, F + SHIFTS + 1], BF16)
        pick = sb("pick", [KP, CH + 1, P], BF16)

        ring = [ps(f"ring{n}", [P, 2, COLS]) for n in range(2)]
        px = ps("px", [P, COLS])
        acc = ps("acc", [P, COLS])
        mid = ps("mid", [P, 2, COLS])
        mid16 = mid[:, :, :].bitcast(BF16)

        gflat = gram[:, :, :, :].rearrange("p a j b -> p (a j b)")
        raw1 = gflat[:, 0:H * F]
        rows = F + SHIFTS - 1
        base = J * TB
        w0r = gflat[:, base:base + rows * F]
        w0c = gflat[:, base + rows * F:base + 2 * rows * F]

        ids_in = [sem(f"ids_in{n}") for n in range(2)]
        gathered = [sem(f"gathered{n}") for n in range(2)]
        w0_in, w1_in, dense_in, mlp_in = sem("w0_in"), sem("w1_in"), sem("dense_in"), sem("mlp_in")
        consts, picks, ones_set = sem("consts"), sem("picks"), sem("ones_set")
        gather_open = sem("gather_open")
        pool_step = sem("pool_step")
        pairs_ready, pair_step = sem("pairs_ready"), sem("pair_step")
        turned = sem("turned")
        kept_act, kept_dve = sem("kept_act"), sem("kept_dve")
        top_ready, rest_ready, mid_ready, low_ready = sem("top_ready"), sem("rest_ready"), sem("mid_ready"), sem("low_ready")
        emb_turned, embT_act, embT_dve = sem("emb_turned"), sem("embT_act"), sem("embT_dve")
        picked, opA_ready, product, hi_ready, lo_ready = sem("picked"), sem("opA_ready"), sem("product"), sem("hi_ready"), sem("lo_ready")
        layer0, x1_ready, x1_turned = sem("layer0"), sem("x1_ready"), sem("x1_turned")
        xTh_ready, xTl_ready, erow_hi, erow_lo = sem("xTh_ready"), sem("xTl_ready"), sem("erow_hi"), sem("erow_lo")
        diag_in, gram_done, gram_kept = sem("diag_in"), sem("gram_done"), sem("gram_kept")
        out1_done, z1_ready, l1_done, h1_ready = sem("out1_done"), sem("z1_ready"), sem("l1_done"), sem("h1_ready")
        l2_done, h2_ready, l3_done, y_ready = sem("l2_done"), sem("h2_ready"), sem("l3_done"), sem("y_ready")
        stored = [sem(f"stored{n}") for n in range(2)]

        ids_t = ids.rearrange("(t p) f -> t p f", p=TB)
        out_t = out.rearrange("(t b) o -> t o b", b=TB)

        block = ctx.enter_context(nc.Block())

        @block.sync
        def _(sp):
            def load_ids(it, n):
                wait(sp, gathered[n], count(it, 16 * F, 0))
                src = ids_t[PAIR * it + n] if isinstance(it, int) else \
                    ids_t[bass.ds(PAIR * it + n, 1)].rearrange("a p f -> p (a f)")
                sp.dma_start(idx[:, n, :], src).then_inc(ids_in[n], 16)

            load_ids(0, 0)
            load_ids(0, 1)
            sp.dma_start(w0r[:, 0:F * F], W0).then_inc(w0_in, 16)
            sp.dma_start(w0r[:, F * F:rows * F], W0[:, 0:(rows - F) * F]).then_inc(w0_in, 16)
            sp.dma_start(raw1, W1).then_inc(w1_in, 16)
            sp.dma_start(dense[:, :, :], dense_ctx.rearrange("(t p) k -> p t k", p=TB)).then_inc(dense_in, 16)
            sp.dma_start(wt1[:, :, :], W_top1[0:2 * P, :].rearrange("(c p) n -> p c n", p=P)).then_inc(mlp_in, 16)
            sp.dma_start(wt1d[:, :], W_top1[2 * P:2 * P + K0, :]).then_inc(mlp_in, 16)
            sp.dma_start(wt2[:, :, :], W_top2.rearrange("(c p) n -> p c n", p=P)).then_inc(mlp_in, 16)
            sp.dma_start(wt3[:, :], W_top3.rearrange("(c p) n -> p (c n)", p=P), allow_slow_non_contiguous=True).then_inc(mlp_in, 16)
            sp.dma_start(bt1[:, :], b_top1.rearrange("(c p) -> p c", p=P), allow_slow_non_contiguous=True).then_inc(mlp_in, 16)
            sp.dma_start(bt2[:, :], b_top2.rearrange("(c p) -> p c", p=P), allow_slow_non_contiguous=True).then_inc(mlp_in, 16)

            def slot(it, q):
                there, k = stage(it, q, 3)
                if q % 2 and there:
                    if isinstance(it, int) and it == 0 and k == 0:
                        sp.wait_ge(ones_set, 3)
                    wait(sp, erow_hi, count(it, PAIR * BLOCKS, k + 1))
                    wait(sp, erow_lo, count(it, PAIR * BLOCKS, k + 1))
                    for b in range(GB):
                        at = slice(D * b, D * b + D)
                        sp.dma_start(diag[at, :, b, :, :].rearrange("p g a j -> p g (a j)").bitcast(F32),
                                     erow[at, :, :, :].rearrange("p g a j -> p g (a j)").bitcast(F32)).then_inc(diag_in, 16)
                if q in (4, 12):
                    n = q // 8
                    if not isinstance(it, int):
                        load_ids(it + 1, n)
                    elif it + 1 < ITERS:
                        load_ids(it + 1, n)
                there, t = stage(it, q, 19, SLOTS)
                if q % SLOTS == 3 and there:
                    wait(sp, y_ready, count(it, PAIR, t + 1))
                    dst = out_t[PAIR * it + t] if isinstance(it, int) else \
                        out_t[bass.ds(PAIR * it + t, 1)].rearrange("a o b -> (a o) b")
                    sp.dma_start(dst, y[:, t % 2, :]).then_inc(stored[t % 2], 16)

            slots(sp, slot)
            for n in range(2):
                sp.wait_ge(stored[n], 16 * TILES // 2)

        @block.gpsimd
        def _(pool):
            pool.memset(id32[:, :], 0.0).then_inc(pool_step, 1)
            pool.memset(id16[:, :], 0.0).then_inc(pool_step, 1)
            pool.memset(match[:, :], 0.0).then_inc(pool_step, 1)
            pool.wait_ge(pool_step, 3)
            for m in (id32, id16):
                pool.affine_select(out=m[:, :], in_=m[:, :], compare_op=ALU.not_equal, fill=1.0, base=0,
                                   pattern=[[-1, P]], channel_multiplier=1).then_inc(consts, 1)
            for n, m in enumerate((-1, 0, 1, 2)):
                pool.wait_ge(pool_step, 3 + n)
                pool.affine_select(out=match[:, :], in_=match[:, :], compare_op=ALU.not_equal, fill=1.0,
                                   base=-F * m, pattern=[[-1, F + SHIFTS + 1]],
                                   channel_multiplier=1).then_inc(pool_step, 1)
            pool.wait_ge(pool_step, 7)

            def gather(it, n):
                wait(pool, low_ready, count(it, PAIR, n - 1))
                wait(pool, ids_in[n], count(it, 16, 16))
                pool.sem_inc(gather_open, 1)
                for f in range(F):
                    pool.indirect_dma_start(
                        out=emb[:, n, f, :], out_offset=None, in_=tables[f],
                        in_offset=bass.IndirectOffsetOnAxis(ap=idx[:, n, f:f + 1], axis=0),
                    ).then_inc(gathered[n], 16)

            for n in range(PAIR):
                gather(0, n)
            with pool.Fori(1, ITERS, 1) as it:
                for n in range(PAIR):
                    gather(it, n)

        @block.scalar
        def _(act):
            def copy(dst, src):
                return act.activation(dst, src, ACT.Copy)

            def split_top(it, n, t):
                wait(act, gathered[n], count(it, 16 * F, 16 * F * (t // 2 + 1)))
                wait(act, emb_turned, count(it, PAIR, t))
                copy(parts[:, :, 0, :], emb[:, n, :, :].rearrange("p f d -> p d f")).then_inc(top_ready, 1)

            def split_mid(it, n, t):
                wait(act, rest_ready, count(it, PAIR, t + 1))
                copy(parts[:, :, 1, :], rest[:, :, :].rearrange("p f d -> p d f")).then_inc(mid_ready, 1)

            def keep_embT(it, n, t):
                wait(act, emb_turned, count(it, PAIR, t + 1))
                src = mid16[0:KP, 0, :].rearrange("p (d b) -> p b d", b=TB)
                copy(embT[0:KP, n, :, 0:D // 2], src).then_inc(embT_act, 1)

            act.wait_ge(turned, 1)
            copy(w0h[0:KP, :, :], mid[0:KP, :, :].rearrange("p a (c h) -> p (a c) h", h=H)[:, 0:CH, :]).then_inc(kept_act, 1)
            act.wait_ge(mlp_in, 16 * 6)
            split_top(0, 0, 0)
            split_mid(0, 0, 0)
            keep_embT(0, 0, 0)

            def slot(it, q):
                there, k = stage(it, q, 0)
                PB = PAIR * BLOCKS
                e0 = 2 * (q % 2)
                r = ENTRIES * k + e0
                if there and q % 2 == 0:
                    wait(act, picked, count(it, ENTRIES * PB, r + 1))
                    wait(act, product, count(it, ENTRIES * PB, ENTRIES * (k - 1)))
                    copy(opA[0:KP, k % 2, :], ring[0][0:KP, 0, :]).then_inc(opA_ready, 1)

                def high(e):
                    n = ENTRIES * k + e
                    wait(act, product, count(it, ENTRIES * PB, n + 1))
                    wait(act, layer0, count(it, ENTRIES * PB, n - ENTRIES + 1))
                    a = 1 if e == 0 else 0
                    copy(hi[0:KP, e, a:2, :], ring[e % 2][0:KP, a:2, :]).then_inc(hi_ready, 1)

                if there:
                    high(e0)
                split, t = stage(it, q, -SLOTS + 5, SLOTS)
                if q % SLOTS == 5 and split:
                    split_top(it, t % 2, t)

                def keep_gram(kg, half):
                    n = 2 * kg + half
                    wait(act, gram_done, count(it, 2 * PB, n + 1))
                    if kg % BLOCKS == 0 and half == 0:
                        wait(act, l1_done, count(it, PAIR, kg // BLOCKS - 1))
                    b0 = (kg % BLOCKS) * BB + half * 2 * GB
                    src = mid[:, :, 0:GB * J].rearrange("p a (b j) -> p j a b", j=J)
                    dst = gram[:, (kg // BLOCKS) % 2, :, b0:b0 + 2 * GB].rearrange("p j (a b) -> p j a b", a=2)
                    copy(dst, src).then_inc(gram_kept, 1)

                gb, kg = stage(it, q, 5)
                if q % 2 and gb:
                    keep_gram(kg, 1)
                if there:
                    high(e0 + 1)
                if q % SLOTS == 5 and split:
                    split_mid(it, t % 2, t)
                done, kx = stage(it, q, 2)
                if q % 2 == 0 and done:
                    wait(act, layer0, count(it, ENTRIES * PB, ENTRIES * (kx + 1)))
                    wait(act, x1_turned, count(it, PB, kx - 1))
                    copy(x1[:, kx % 2, :], px[:, :]).then_inc(x1_ready, 1)
                done, kx = stage(it, q, 3)
                if q % 2 and done:
                    wait(act, x1_turned, count(it, PB, kx + 1))
                    copy(erow[:, :, 0, 0:F], mid[:, 1, 0:GROUPS * J].rearrange("p (g j) -> p g j", j=J)[:, :, 0:F]).then_inc(erow_hi, 1)
                    copy(xTh[:, :, :], mid[:, 0, :].rearrange("p (g h) -> p g h", h=H)).then_inc(xTh_ready, 1)
                turn, t = stage(it, q, -SLOTS + 6, SLOTS)
                if q % SLOTS == 6 and turn:
                    keep_embT(it, t % 2, t)
                ga, kg = stage(it, q, 4)
                if q % 2 == 0 and ga:
                    keep_gram(kg, 0)

                there, t = stage(it, q, 16, SLOTS)
                if q % SLOTS == 0 and there:
                    wait(act, out1_done, count(it, PAIR, t + 1))
                    copy(z1[:, :], acc[:, 0:TB]).then_inc(z1_ready, 1)
                if q % SLOTS == 1 and there:
                    wait(act, l1_done, count(it, PAIR, t + 1))
                    for m in range(N1 // P):
                        op = act.activation(h1[:, m, :], acc[:, m * TB:(m + 1) * TB], ACT.Relu, bias=bt1[:, m:m + 1])
                    op.then_inc(h1_ready, 1)
                if q % SLOTS == 2 and there:
                    wait(act, l2_done, count(it, PAIR, t + 1))
                    for m in range(N2 // P):
                        op = act.activation(h2[:, m, :], acc[:, m * TB:(m + 1) * TB], ACT.Relu, bias=bt2[:, m:m + 1])
                    op.then_inc(h2_ready, 1)
                if q % SLOTS == 3 and there:
                    wait(act, l3_done, count(it, PAIR, t + 1))
                    wait(act, stored[t % 2], count(it, 16, 16 * (t // 2)))
                    copy(y[:, t % 2, :], acc[0:1, 0:TB]).then_inc(y_ready, 1)

            slots(act, slot)

        @block.vector
        def _(dve):
            def split_rest(it, n, t):
                wait(dve, top_ready, count(it, PAIR, t + 1))
                dve.tensor_tensor(rest[:, :, :], emb[:, n, :, :], parts[:, :, 0, :].rearrange("p d f -> p f d"),
                                  ALU.subtract).then_inc(rest_ready, 1)

            def split_low(it, n, t):
                wait(dve, mid_ready, count(it, PAIR, t + 1))
                dve.tensor_tensor(parts[:, :, 2, :], rest[:, :, :].rearrange("p f d -> p d f"), parts[:, :, 1, :],
                                  ALU.subtract).then_inc(low_ready, 1)

            def keep_embT(it, n, t):
                wait(dve, emb_turned, count(it, PAIR, t + 1))
                src = mid16[0:KP, 1, :].rearrange("p (d b) -> p b d", b=TB)
                dve.tensor_copy(embT[0:KP, n, :, D // 2:D], src).then_inc(embT_dve, 1)

            dve.memset(diag[:, :, :, :, :].bitcast(F32), 0.0).then_inc(ones_set, 1)
            dve.memset(erow[:, :, 0, F:J].bitcast(F32), 1.0).then_inc(ones_set, 1)
            dve.memset(erow[:, :, 1, F:J].bitcast(F32), 0.0).then_inc(ones_set, 1)
            dve.memset(pick[:, :, :], 0.0).then_inc(pair_step, 1)
            dve.memset(pairs[:, :, :], 0.0).then_inc(pair_step, 1)
            dve.wait_ge(pool_step, 7)
            dve.wait_ge(pair_step, 2)
            for r in range(R):
                at = slice(F * r, F * r + F)
                dve.tensor_copy(pick[:, 0, at], match[:, 0:F]).then_inc(picks, 1)
                for c in range(CH):
                    dve.tensor_copy(pick[:, 1 + c, at], match[:, R * c + r:R * c + r + F]).then_inc(picks, 1)
            dve.wait_ge(w0_in, 32)
            dve.tensor_copy(w0c.rearrange("p (i x) -> p i x", x=rows)[:, :, 0:F],
                            w0r[:, 0:F * F].rearrange("p (i x) -> p i x", x=F)).then_inc(pair_step, 1)
            dve.tensor_copy(w0c.rearrange("p (i x) -> p i x", x=rows)[:, :, F:rows],
                            w0r[:, 0:F * F].rearrange("p (i x) -> p i x", x=F)[:, :, 0:rows - F]).then_inc(pair_step, 1)
            dve.tensor_copy(pairs[:, 0, :], w0r[:, 0:(F - 1) * J + 1:J]).then_inc(pair_step, 1)
            dve.wait_ge(pair_step, 5)
            for s in range(1, SHIFTS):
                op = dve.tensor_tensor(pairs[:, s, :], w0c[:, s:s + (F - 1) * (rows + 1) + 1:rows + 1],
                                       w0r[:, s * F:s * F + (F - 1) * J + 1:J], ALU.add)
            op.then_inc(pairs_ready, 1)
            dve.wait_ge(kept_act, 1)
            dve.tensor_tensor(w0l[0:KP, :, :], mid[0:KP, :, :].rearrange("p a (c h) -> p (a c) h", h=H)[:, 0:CH, :],
                              w0h[0:KP, :, :].bitcast(F32), ALU.subtract).then_inc(kept_dve, 1)
            turns = 1
            for j in range(0, F, 8):
                n = min(8, F - j)
                turns += 1
                dve.wait_ge(turned, turns)
                dve.tensor_copy(w1T[:, j:j + n, :], mid[:, :, :].rearrange("p a (c h) -> p (a c) h", h=H)[:, 0:n, :]).then_inc(kept_dve, 1)
            for t in range(0, TILES, 8):
                turns += 1
                dve.wait_ge(turned, turns)
                dve.tensor_copy(denseT[:, t * TB:(t + 8) * TB], mid[0:K0, :, :].rearrange("p a b -> p (a b)")).then_inc(kept_dve, 1)
            split_rest(0, 0, 0)
            split_low(0, 0, 0)
            keep_embT(0, 0, 0)

            def slot(it, q):
                PB = PAIR * BLOCKS
                there, k = stage(it, q, 0)
                e0 = 2 * (q % 2)

                def multiply(e):
                    n = ENTRIES * k + e
                    wait(dve, picked, count(it, ENTRIES * PB, n + 1))
                    if e == 0:
                        wait(dve, opA_ready, count(it, PB, k + 1))
                        a, by = 1, opA[0:KP, k % 2, :]
                        dve.tensor_tensor(ring[0][0:KP, 1, :], ring[0][0:KP, 1, :], by, ALU.mult).then_inc(product, 1)
                    else:
                        by = opA[0:KP, k % 2, :].rearrange("p (a n) -> p a n", a=1).broadcast_to([KP, 2, COLS])
                        dve.tensor_tensor(ring[e % 2][0:KP, :, :], ring[e % 2][0:KP, :, :], by, ALU.mult).then_inc(product, 1)

                def low(e):
                    n = ENTRIES * k + e
                    wait(dve, hi_ready, count(it, ENTRIES * PB, n + 1))
                    wait(dve, layer0, count(it, ENTRIES * PB, n - ENTRIES + 1))
                    a = 1 if e == 0 else 0
                    dve.tensor_tensor(lo[0:KP, e, a:2, :], ring[e % 2][0:KP, a:2, :],
                                      hi[0:KP, e, a:2, :].bitcast(F32), ALU.subtract).then_inc(lo_ready, 1)

                if there:
                    multiply(e0)
                    multiply(e0 + 1)
                split, t = stage(it, q, -SLOTS + 5, SLOTS)
                if q % SLOTS == 5 and split:
                    split_rest(it, t % 2, t)
                if there:
                    low(e0)
                    low(e0 + 1)
                done, kx = stage(it, q, 3)
                if q % 2 and done:
                    wait(dve, erow_hi, count(it, PB, kx + 1))
                    dve.tensor_tensor(erow[:, :, 1, 0:F], mid[:, 1, 0:GROUPS * J].rearrange("p (g j) -> p g j", j=J)[:, :, 0:F],
                                      erow[:, :, 0, 0:F].bitcast(F32), ALU.subtract).then_inc(erow_lo, 1)
                    wait(dve, xTh_ready, count(it, PB, kx + 1))
                    dve.tensor_tensor(xTl[:, :, :], mid[:, 0, :].rearrange("p (g h) -> p g h", h=H),
                                      xTh[:, :, :].bitcast(F32), ALU.subtract).then_inc(xTl_ready, 1)
                if q % SLOTS == 5 and split:
                    split_low(it, t % 2, t)
                turn, t = stage(it, q, -SLOTS + 6, SLOTS)
                if q % SLOTS == 6 and turn:
                    keep_embT(it, t % 2, t)

            slots(dve, slot)

        @block.tensor
        def _(pe):
            def turn_embedding(it, n, t):
                for d in range(D):
                    if d == 0:
                        wait(pe, low_ready, count(it, PAIR, t + 1))
                    op = pe.transpose(mid16[0:KP, d // 8, (d % 8) * TB:(d % 8 + 1) * TB],
                                      parts[:, d, :, :].rearrange("p a f -> p (a f)"), id16[:, :])
                op.then_inc(emb_turned, 1)

            pe.wait_ge(consts, 2)
            pe.wait_ge(pairs_ready, 1)
            for c in range(CH):
                op = pe.transpose(mid[0:KP, c // 4, (c % 4) * H:(c % 4 + 1) * H],
                                  pairs[:, R * c:R * c + R, :].rearrange("p s i -> p (s i)"), id32[:, :])
            op.then_inc(turned, 1)
            pe.wait_ge(w1_in, 16)
            for n, j0 in enumerate(range(0, F, 8)):
                pe.wait_ge(kept_dve, n + 1)
                for j in range(j0, min(j0 + 8, F)):
                    c = j - j0
                    op = pe.transpose(mid[:, c // 4, (c % 4) * H:(c % 4 + 1) * H], raw1[:, j:j + (H - 1) * F + 1:F], id32[:, :])
                op.then_inc(turned, 1)
            pe.wait_ge(dense_in, 16)
            for m, t0 in enumerate(range(0, TILES, 8)):
                pe.wait_ge(kept_dve, n + 2 + m)
                for c in range(8):
                    op = pe.transpose(mid[0:K0, c // 4, (c % 4) * TB:(c % 4 + 1) * TB], dense[:, t0 + c, :], id32[:, :])
                op.then_inc(turned, 1)
            pe.wait_ge(kept_dve, n + 3 + m)
            turn_embedding(0, 0, 0)
            pe.wait_ge(picks, R * (CH + 1))
            pe.wait_ge(mlp_in, 16 * 6)

            def slot(it, q):
                PB = PAIR * BLOCKS

                def choose(k, e):
                    n = ENTRIES * k + e
                    if k % BLOCKS == 0 and e == 0:
                        wait(pe, embT_act, count(it, PAIR, k // BLOCKS + 1))
                        wait(pe, embT_dve, count(it, PAIR, k // BLOCKS + 1))
                    wait(pe, lo_ready, count(it, ENTRIES * PB, n - 1))
                    b0 = (k % BLOCKS) * BB
                    cols = embT[0:KP, (k // BLOCKS) % 2, b0:b0 + BB, :].rearrange("p b d -> p (b d)")
                    for a in range(2):
                        op = pe.matmul(ring[e % 2][:, a, :], pick[:, 2 * e + a, :], cols, start=True, stop=True)
                    op.then_inc(picked, 1)

                def convolve(k, e):
                    n = ENTRIES * k + e
                    if e == 0:
                        wait(pe, x1_ready, count(it, PB, k))
                    chunks = [(a, 2 * e + a - 1) for a in range(2) if 2 * e + a]
                    wait(pe, hi_ready, count(it, ENTRIES * PB, n + 1))
                    for a, c in chunks:
                        pe.matmul(px[:, :], w0h[0:KP, c, :], hi[0:KP, e, a, :], start=(c == 0), stop=False)
                        pe.matmul(px[:, :], w0l[0:KP, c, :], hi[0:KP, e, a, :], start=False, stop=False)
                    wait(pe, lo_ready, count(it, ENTRIES * PB, n + 1))
                    for a, c in chunks:
                        op = pe.matmul(px[:, :], w0h[0:KP, c, :], lo[0:KP, e, a, :], start=False, stop=(c == CH - 1))
                    op.then_inc(layer0, 1)

                def correlate(kg, half):
                    for a in range(2):
                        g = 2 * half + a
                        terms = ((xTh, 0), (xTl, 0), (xTh, 1))
                        for m, (x, part) in enumerate(terms):
                            op = pe.matmul(mid[:, a, 0:GB * J], x[:, g, :], diag[:, g, :, part, :],
                                           start=(m == 0), stop=(m == len(terms) - 1))
                    op.then_inc(gram_done, 1)

                def second(t, part):
                    if part == 0:
                        wait(pe, gram_kept, count(it, 2 * PB, 2 * BLOCKS * (t + 1)))
                        wait(pe, y_ready, count(it, PAIR, t))
                    for j in range(part * OUT1_J, min(F, (part + 1) * OUT1_J)):
                        op = pe.matmul(acc[:, 0:TB], w1T[:, j, :], gram[:, t % 2, j, :], start=(j == 0), stop=(j == F - 1))
                    if part == OUT1_STEPS - 1:
                        op.then_inc(out1_done, 1)

                there, k = stage(it, q, 0)
                last, kl = stage(it, q, 1)
                e0 = 2 * (q % 2)
                el = 2 - e0
                if there:
                    choose(k, e0)
                if last:
                    convolve(kl, el)
                if there:
                    choose(k, e0 + 1)
                turn, t = stage(it, q, -SLOTS + 6, SLOTS)
                if q % SLOTS == 6 and turn:
                    _, kx = stage(it, q, 4)
                    wait(pe, xTl_ready, count(it, PB, kx + 1))
                    turn_embedding(it, t % 2, t)
                gb, kg = stage(it, q, 5)
                if q % 2 and gb:
                    wait(pe, gram_kept, count(it, 2 * PB, 2 * kg + 1))
                    correlate(kg, 1)
                if last:
                    convolve(kl, el + 1)
                ga, kg = stage(it, q, 4)
                if q % 2 == 0 and ga:
                    wait(pe, diag_in, count(it, 16 * GB * PB, 16 * GB * (kg + 1)))
                    wait(pe, xTh_ready, count(it, PB, kg + 1))
                    wait(pe, xTl_ready, count(it, PB, kg + 1))
                    if q % SLOTS == 6 and turn:
                        wait(pe, embT_act, count(it, PAIR, t + 1))
                        wait(pe, embT_dve, count(it, PAIR, t + 1))
                    correlate(kg, 0)
                done, kx = stage(it, q, 3)
                if q % 2 and done:
                    wait(pe, x1_ready, count(it, PB, kx + 1))
                    wait(pe, gram_kept, count(it, 2 * PB, 2 * kx))
                    b0 = (kx % BLOCKS) * BB
                    for g in range(GROUPS):
                        pe.transpose(mid[:, 0, g * H:(g + 1) * H], x1[:, kx % 2, g * P:(g + 1) * P], id32[:, :])
                    for g in range(GROUPS):
                        cols = embT[0:KP, (kx // BLOCKS) % 2, b0 + g * GB:b0 + (g + 1) * GB, :].rearrange("p b d -> p (b d)")
                        op = pe.matmul(mid[:, 1, g * J:g * J + F], cols, match[:, 0:F], start=True, stop=True)
                    op.then_inc(x1_turned, 1)

                there, t = stage(it, q, 12, SLOTS)
                if q % SLOTS >= 4 and there:
                    second(t, q % SLOTS - 4)
                there, t = stage(it, q, 16, SLOTS)
                if q % SLOTS == 0 and there:
                    second(t, 4)
                if q % SLOTS == 1 and there:
                    wait(pe, z1_ready, count(it, PAIR, t + 1))
                    at = slice((PAIR * it + t) * TB, (PAIR * it + t + 1) * TB) if isinstance(it, int) else \
                        bass.ds(it * (PAIR * TB) + t * TB, TB)
                    for m in range(N1 // P):
                        w = slice(m * P, (m + 1) * P)
                        o = acc[:, m * TB:(m + 1) * TB]
                        pe.matmul(o, wt1[:, 0, w], gram[:, t % 2, F, :], start=True, stop=False)
                        pe.matmul(o, wt1[:, 1, w], z1[:, :], start=False, stop=False)
                        op = pe.matmul(o, wt1d[:, w], denseT[:, at], start=False, stop=True)
                    op.then_inc(l1_done, 1)
                if q % SLOTS == 2 and there:
                    wait(pe, h1_ready, count(it, PAIR, t + 1))
                    for m in range(N2 // P):
                        for c in range(N1 // P):
                            op = pe.matmul(acc[:, m * TB:(m + 1) * TB], wt2[:, c, m * P:(m + 1) * P], h1[:, c, :],
                                           start=(c == 0), stop=(c == N1 // P - 1))
                    op.then_inc(l2_done, 1)
                if q % SLOTS == 3 and there:
                    wait(pe, h2_ready, count(it, PAIR, t + 1))
                    for c in range(N2 // P):
                        op = pe.matmul(acc[0:1, 0:TB], wt3[:, c:c + 1], h2[:, c, :], start=(c == 0), stop=(c == N2 // P - 1))
                    op.then_inc(l3_done, 1)

            slots(pe, slot)


def kernel(**inputs):
    import numpy as _np
    import concourse.bacc as _bacc
    from concourse.bass_utils import run_bass_kernel_spmd as _run

    nc = _bacc.Bacc("TRN2", target_bir_lowering=False, num_devices=1)
    arrays, dram = {}, {}
    names = ["dense_ctx", "ids"] + TABLES + ["W_top1", "b_top1", "W_top2", "b_top2", "W_top3", "L0_rec_W0", "L0_rec_W1"]
    for name in names:
        a = _np.ascontiguousarray(inputs[name])
        arrays[f"in_{name}"] = a
        dram[name] = nc.dram_tensor(f"in_{name}", a.shape, mybir.dt.from_np(a.dtype), kind="ExternalInput").ap()
    y = nc.dram_tensor("out_y", (B, 1), F32, kind="ExternalOutput").ap()
    build(nc, dram["dense_ctx"], dram["ids"], [dram[n] for n in TABLES], dram["W_top1"], dram["b_top1"],
          dram["W_top2"], dram["b_top2"], dram["W_top3"], dram["L0_rec_W0"], dram["L0_rec_W1"], y)
    r = _run(nc, [arrays], core_ids=[0])
    return r.results[0]["out_y"]
```

```python
from contextlib import ExitStack

import concourse.bass as bass
from concourse import mybir

ALU = mybir.AluOpType
ACT = mybir.ActivationFunctionType
F32 = mybir.dt.float32
F32R = mybir.dt.float32r
BF16 = mybir.dt.bfloat16
I32 = mybir.dt.int32

B, F, D, H = 2048, 39, 16, 128
K0, N1, N2 = 16, 512, 256
P = 128
TB = P
TILES = B // TB
COLS = 512
BB = COLS // D
BLOCKS = TB // BB
GB = P // D
GROUPS = BB // GB
SHIFTS = (F + 1) // 2
OFFSETS = ((0, 2, 0, 3, 6), (0, 5, 14, 16, 18), (0, 7, 15, 17, 19))
R = len(OFFSETS)
KP = R * F
OPS = len(OFFSETS[0])
ENTRIES = OPS - 1
CHUNKS = [(0, 1)] + [(m, n) for n in range(2, OPS) for m in range(2)]
CH = len(CHUNKS)
WRAP = F + max(map(max, OFFSETS))
J = F + 1
TABLES = [f"tbl_{f}" for f in range(F)]
SLOTS = 2 * BLOCKS
PAIR = 2
S_IT = PAIR * SLOTS
SPLIT = 3
TAIL = 14
ITERS = TILES // PAIR
OUT1_STEPS = 5
OUT1_J = 8
assert ENTRIES == 4 and F % 2 == 1


def runs():
    seen = {}
    for c, (m, n) in enumerate(CHUNKS):
        for r in range(R):
            a, b = OFFSETS[r][m], OFFSETS[r][n]
            seen.setdefault(min((a - b) % F, (b - a) % F), (c, r, a, b))
    assert sorted(seen) == list(range(SHIFTS))
    return [(c, r, shift, a, b) for shift, (c, r, a, b) in seen.items()]


def count(it, per, local):
    return it * per + local


def wait(eng, sem, value):
    if not isinstance(value, int) or value > 0:
        eng.wait_ge(sem, value)


def slots(eng, emit):
    for q in range(S_IT):
        emit(0, q)
    with eng.Fori(1, ITERS - 1, 1) as it:
        for q in range(S_IT):
            emit(it, q)
    for it in (ITERS - 1, ITERS):
        for q in range(S_IT if it < ITERS else TAIL):
            emit(it, q)


def stage(it, q, lag, every=2):
    local = (q - lag) // every
    if isinstance(it, int):
        n = it * (S_IT // every) + local
        return 0 <= n < TILES * SLOTS // every, local
    return True, local


def ahead(it, q, at, late):
    there, t = stage(it, q, at - SLOTS, SLOTS)
    first = isinstance(it, int) and it * PAIR + t <= PAIR
    return there and q % SLOTS == (late if first else at), t


def build(nc, dense_ctx, ids, tables, W_top1, b_top1, W_top2, b_top2, W_top3, W0, W1, out):
    with ExitStack() as ctx:
        def sb(name, shape, dt=F32):
            return ctx.enter_context(nc.sbuf_tensor(name, shape, dt))

        def ps(name, shape):
            return ctx.enter_context(nc.psum_tensor(name, shape, F32))

        def sem(name):
            return ctx.enter_context(nc.semaphore(name))

        idx = sb("idx", [P, 2, F], I32)
        emb = sb("emb", [P, 2, F, D])
        rest = sb("rest", [P, F, D])
        parts = sb("parts", [P, D, 3, F], BF16)
        embT = sb("embT", [P, 2, TB, D], BF16)
        opA = sb("opA", [P, 2, 2, COLS])
        hi = sb("hi", [P, ENTRIES, 2, COLS], F32R)
        lo = sb("lo", [P, ENTRIES, 2, COLS], F32R)
        x1 = sb("x1", [P, 2, COLS])
        xTh = sb("xTh", [P, 2, GROUPS, H], F32R)
        xTl = sb("xTl", [P, 2, GROUPS, H], F32R)
        erow = sb("erow", [P, 2, GROUPS, 2, J], F32R)
        diag = sb("diag", [P, 2, GROUPS, GB, 2, J], F32R)
        gram = sb("gram", [P, 2, J, TB])
        w0h = sb("w0h", [P, CH, H], F32R)
        w0l = sb("w0l", [P, CH, H], F32R)
        w1T = sb("w1T", [P, F, H])
        wt1 = sb("wt1", [P, 2, N1])
        wt1d = sb("wt1d", [K0, N1])
        wt2 = sb("wt2", [P, N1 // P, N2])
        wt3 = sb("wt3", [P, N2 // P])
        bt1 = sb("bt1", [P, N1 // P])
        bt2 = sb("bt2", [P, N2 // P])
        pairs = sb("pairs", [P, CH, R, F])
        dense = sb("dense", [P, TILES, K0])
        denseT = sb("denseT", [K0, B])
        z1 = sb("z1", [P, TB])
        h1 = sb("h1", [P, N1 // P, TB])
        h2 = sb("h2", [P, N2 // P, TB])
        y = sb("y", [1, 2, TB])
        id32 = sb("id32", [P, P])
        id16 = sb("id16", [P, P], BF16)
        match = sb("match", [KP, WRAP], BF16)
        pick = sb("pick", [KP, OPS, P], BF16)

        ring = [ps(f"ring{n}", [P, 2, COLS]) for n in range(2)]
        px = ps("px", [P, COLS])
        acc = ps("acc", [P, COLS])
        mid = ps("mid", [P, 2, COLS])
        mid16 = mid[:, :, :].bitcast(BF16)

        gflat = gram[:, :, :, :].rearrange("p a j b -> p (a j b)")
        raw1 = gflat[:, 0:H * F]
        raw0 = gflat[:, J * TB:J * TB + WRAP * WRAP]
        raw0v = raw0.rearrange("p (i j) -> p i j", j=WRAP)

        ids_in = [sem(f"ids_in{n}") for n in range(2)]
        gathered = [sem(f"gathered{n}") for n in range(2)]
        w0_in, w1_in, dense_in, mlp_in = sem("w0_in"), sem("w1_in"), sem("dense_in"), sem("mlp_in")
        consts, picks, ones_set = sem("consts"), sem("picks"), sem("ones_set")
        gather_open = sem("gather_open")
        pool_step = sem("pool_step")
        pairs_ready, pair_step = sem("pairs_ready"), sem("pair_step")
        turned = sem("turned")
        kept_act, kept_dve = sem("kept_act"), sem("kept_dve")
        top_ready, rest_ready, mid_ready, low_ready = sem("top_ready"), sem("rest_ready"), sem("mid_ready"), sem("low_ready")
        emb_turned, embT_act, embT_dve = sem("emb_turned"), sem("embT_act"), sem("embT_dve")
        picked, opA_ready, product, hi_ready, lo_ready = sem("picked"), sem("opA_ready"), sem("product"), sem("hi_ready"), sem("lo_ready")
        layer0, x1_ready, x1_turned = sem("layer0"), sem("x1_ready"), sem("x1_turned")
        xTh_ready, xTl_ready, erow_hi, erow_lo = sem("xTh_ready"), sem("xTl_ready"), sem("erow_hi"), sem("erow_lo")
        diag_in = [sem(f"diag_in{n}") for n in range(2)]
        gram_done, gram_kept = sem("gram_done"), sem("gram_kept")
        out1_done, z1_ready, l1_done, h1_ready = sem("out1_done"), sem("z1_ready"), sem("l1_done"), sem("h1_ready")
        l2_done, h2_ready, l3_done, y_ready = sem("l2_done"), sem("h2_ready"), sem("l3_done"), sem("y_ready")
        stored = [sem(f"stored{n}") for n in range(2)]

        ids_t = ids.rearrange("(t p) f -> t p f", p=TB)
        out_t = out.rearrange("(t b) o -> t o b", b=TB)

        block = ctx.enter_context(nc.Block())

        @block.sync
        def _(sp):
            def load_ids(it, n):
                wait(sp, gathered[n], count(it, 16 * F, 0))
                src = ids_t[PAIR * it + n] if isinstance(it, int) else \
                    ids_t[bass.ds(PAIR * it + n, 1)].rearrange("a p f -> p (a f)")
                sp.dma_start(idx[:, n, :], src).then_inc(ids_in[n], 16)

            load_ids(0, 0)
            load_ids(0, 1)
            sp.dma_start(raw0v[:, 0:F, 0:F], W0.rearrange("h (i j) -> h i j", j=F)).then_inc(w0_in, 16)
            sp.dma_start(raw1, W1).then_inc(w1_in, 16)
            sp.dma_start(dense[:, :, :], dense_ctx.rearrange("(t p) k -> p t k", p=TB)).then_inc(dense_in, 16)
            sp.dma_start(wt1[:, :, :], W_top1[0:2 * P, :].rearrange("(c p) n -> p c n", p=P)).then_inc(mlp_in, 16)
            sp.dma_start(wt1d[:, :], W_top1[2 * P:2 * P + K0, :]).then_inc(mlp_in, 16)
            sp.dma_start(wt2[:, :, :], W_top2.rearrange("(c p) n -> p c n", p=P)).then_inc(mlp_in, 16)
            sp.dma_start(wt3[:, :], W_top3.rearrange("(c p) n -> p (c n)", p=P), allow_slow_non_contiguous=True).then_inc(mlp_in, 16)
            sp.dma_start(bt1[:, :], b_top1.rearrange("(c p) -> p c", p=P), allow_slow_non_contiguous=True).then_inc(mlp_in, 16)
            sp.dma_start(bt2[:, :], b_top2.rearrange("(c p) -> p c", p=P), allow_slow_non_contiguous=True).then_inc(mlp_in, 16)

            def slot(it, q):
                there, k = stage(it, q, 3)
                if q % 2 and there:
                    if isinstance(it, int) and it == 0 and k == 0:
                        sp.wait_ge(ones_set, 3)
                    wait(sp, erow_hi, count(it, PAIR * BLOCKS, k + 1))
                    wait(sp, erow_lo, count(it, PAIR * BLOCKS, k + 1))
                    for b in range(GB):
                        at = slice(D * b, D * b + D)
                        sp.dma_start(diag[at, k % 2, :, b, :, :].rearrange("p g a j -> p g (a j)").bitcast(F32),
                                     erow[at, k % 2, :, :, :].rearrange("p g a j -> p g (a j)").bitcast(F32)).then_inc(diag_in[k % 2], 16)
                if q % SLOTS == 0:
                    n = q // SLOTS
                    if not isinstance(it, int):
                        load_ids(it + 1, n)
                    elif it + 1 < ITERS:
                        load_ids(it + 1, n)
                there, t = stage(it, q, 21, SLOTS)
                if q % SLOTS == 5 and there:
                    wait(sp, y_ready, count(it, PAIR, t + 1))
                    dst = out_t[PAIR * it + t] if isinstance(it, int) else \
                        out_t[bass.ds(PAIR * it + t, 1)].rearrange("a o b -> (a o) b")
                    sp.dma_start(dst, y[:, t % 2, :]).then_inc(stored[t % 2], 16)

            slots(sp, slot)
            for n in range(2):
                sp.wait_ge(stored[n], 16 * TILES // 2)

        @block.gpsimd
        def _(pool):
            pool.memset(id32[:, :], 0.0).then_inc(pool_step, 1)
            pool.memset(id16[:, :], 0.0).then_inc(pool_step, 1)
            pool.memset(match[:, :], 0.0).then_inc(pool_step, 1)
            pool.wait_ge(pool_step, 3)
            for m in (id32, id16):
                pool.affine_select(out=m[:, :], in_=m[:, :], compare_op=ALU.not_equal, fill=1.0, base=0,
                                   pattern=[[-1, P]], channel_multiplier=1).then_inc(consts, 1)
            for n, m in enumerate((-1, 0, 1, 2)):
                pool.wait_ge(pool_step, 3 + n)
                pool.affine_select(out=match[:, :], in_=match[:, :], compare_op=ALU.not_equal, fill=1.0,
                                   base=-F * m, pattern=[[-1, WRAP]],
                                   channel_multiplier=1).then_inc(pool_step, 1)
            pool.wait_ge(pool_step, 7)

            def gather(it, n):
                wait(pool, low_ready, count(it, PAIR, n - 1))
                wait(pool, ids_in[n], count(it, 16, 16))
                pool.sem_inc(gather_open, 1)
                for f in range(F):
                    pool.indirect_dma_start(
                        out=emb[:, n, f, :], out_offset=None, in_=tables[f],
                        in_offset=bass.IndirectOffsetOnAxis(ap=idx[:, n, f:f + 1], axis=0),
                    ).then_inc(gathered[n], 16)

            for n in range(PAIR):
                gather(0, n)
            with pool.Fori(1, ITERS, 1) as it:
                for n in range(PAIR):
                    gather(it, n)

        @block.scalar
        def _(act):
            def copy(dst, src):
                return act.activation(dst, src, ACT.Copy)

            def split_top(it, n, t):
                wait(act, gathered[n], count(it, 16 * F, 16 * F * (t // 2 + 1)))
                wait(act, emb_turned, count(it, PAIR, t))
                copy(parts[:, :, 0, :], emb[:, n, :, :].rearrange("p f d -> p d f")).then_inc(top_ready, 1)

            def split_mid(it, n, t):
                wait(act, rest_ready, count(it, PAIR, t + 1))
                copy(parts[:, :, 1, :], rest[:, :, :].rearrange("p f d -> p d f")).then_inc(mid_ready, 1)

            def keep_embT(it, n, t):
                wait(act, emb_turned, count(it, PAIR, t + 1))
                src = mid16[0:KP, 0, :].rearrange("p (d b) -> p b d", b=TB)
                copy(embT[0:KP, n, :, 0:D // 2], src).then_inc(embT_act, 1)

            act.wait_ge(turned, 1)
            copy(w0h[0:KP, :, :], mid[0:KP, :, :].rearrange("p a (c h) -> p (a c) h", h=H)[:, 0:CH, :]).then_inc(kept_act, 1)
            act.wait_ge(mlp_in, 16 * 6)
            split_top(0, 0, 0)
            split_mid(0, 0, 0)
            keep_embT(0, 0, 0)

            def slot(it, q):
                there, k = stage(it, q, 0)
                PB = PAIR * BLOCKS
                e0 = 2 * (q % 2)
                r = ENTRIES * k + e0
                if there and q % 2 == 0:
                    wait(act, picked, count(it, ENTRIES * PB, r + 1))
                    wait(act, product, count(it, ENTRIES * PB, ENTRIES * (k - 1)))
                    copy(opA[0:KP, k % 2, :, :], ring[0][0:KP, :, :]).then_inc(opA_ready, 1)

                def high(e):
                    n = ENTRIES * k + e
                    wait(act, product, count(it, ENTRIES * PB, n + 1))
                    wait(act, layer0, count(it, ENTRIES * PB, n - ENTRIES + 1))
                    a = 1 if e == 0 else 0
                    copy(hi[0:KP, e, a:2, :], ring[e % 2][0:KP, a:2, :]).then_inc(hi_ready, 1)

                def keep_gram(kg, half):
                    n = 2 * kg + half
                    wait(act, gram_done, count(it, 2 * PB, n + 1))
                    if kg % BLOCKS == 0 and half == 0:
                        wait(act, l1_done, count(it, PAIR, kg // BLOCKS - 1))
                    b0 = (kg % BLOCKS) * BB + half * 2 * GB
                    src = mid[:, :, 0:GB * J].rearrange("p a (b j) -> p j a b", j=J)
                    dst = gram[:, (kg // BLOCKS) % 2, :, b0:b0 + 2 * GB].rearrange("p j (a b) -> p j a b", a=2)
                    copy(dst, src).then_inc(gram_kept, 1)

                gb, kg = stage(it, q, 7)
                if q % 2 and gb:
                    keep_gram(kg, 1)
                split, t = ahead(it, q, SPLIT, SLOTS - 1)
                if split:
                    split_top(it, t % 2, t)
                turn, t = ahead(it, q, SLOTS - 2, SLOTS - 1)
                if turn and q % SLOTS == SLOTS - 2:
                    keep_embT(it, t % 2, t)
                if there:
                    high(e0)
                split, t = ahead(it, q, SPLIT + 1, SLOTS - 1)
                if split:
                    split_mid(it, t % 2, t)
                if there:
                    high(e0 + 1)
                done, kx = stage(it, q, 2)
                if q % 2 == 0 and done:
                    wait(act, layer0, count(it, ENTRIES * PB, ENTRIES * (kx + 1)))
                    wait(act, x1_turned, count(it, PB, kx - 1))
                    copy(x1[:, kx % 2, :], px[:, :]).then_inc(x1_ready, 1)
                done, kx = stage(it, q, 3)
                if q % 2 and done:
                    wait(act, x1_turned, count(it, PB, kx + 1))
                    wait(act, diag_in[kx % 2], count(it, 16 * GB * PB // 2, 16 * GB * (kx // 2)))
                    copy(erow[:, kx % 2, :, 0, 0:F], mid[:, 1, 0:GROUPS * J].rearrange("p (g j) -> p g j", j=J)[:, :, 0:F]).then_inc(erow_hi, 1)
                    copy(xTh[:, kx % 2, :, :], mid[:, 0, :].rearrange("p (g h) -> p g h", h=H)).then_inc(xTh_ready, 1)
                ga, kg = stage(it, q, 6)
                if q % 2 == 0 and ga:
                    keep_gram(kg, 0)
                turn, t = ahead(it, q, SLOTS - 2, SLOTS - 1)
                if turn and q % SLOTS == SLOTS - 1:
                    keep_embT(it, t % 2, t)

                there, t = stage(it, q, 18, SLOTS)
                if q % SLOTS == 2 and there:
                    wait(act, out1_done, count(it, PAIR, t + 1))
                    copy(z1[:, :], acc[:, 0:TB]).then_inc(z1_ready, 1)
                if q % SLOTS == 3 and there:
                    wait(act, l1_done, count(it, PAIR, t + 1))
                    for m in range(N1 // P):
                        op = act.activation(h1[:, m, :], acc[:, m * TB:(m + 1) * TB], ACT.Relu, bias=bt1[:, m:m + 1])
                    op.then_inc(h1_ready, 1)
                if q % SLOTS == 4 and there:
                    wait(act, l2_done, count(it, PAIR, t + 1))
                    for m in range(N2 // P):
                        op = act.activation(h2[:, m, :], acc[:, m * TB:(m + 1) * TB], ACT.Relu, bias=bt2[:, m:m + 1])
                    op.then_inc(h2_ready, 1)
                if q % SLOTS == 5 and there:
                    wait(act, l3_done, count(it, PAIR, t + 1))
                    wait(act, stored[t % 2], count(it, 16, 16 * (t // 2)))
                    copy(y[:, t % 2, :], acc[0:1, 0:TB]).then_inc(y_ready, 1)

            slots(act, slot)

        @block.vector
        def _(dve):
            def split_rest(it, n, t):
                wait(dve, top_ready, count(it, PAIR, t + 1))
                dve.tensor_tensor(rest[:, :, :], emb[:, n, :, :], parts[:, :, 0, :].rearrange("p d f -> p f d"),
                                  ALU.subtract).then_inc(rest_ready, 1)

            def split_low(it, n, t):
                wait(dve, mid_ready, count(it, PAIR, t + 1))
                dve.tensor_tensor(parts[:, :, 2, :], rest[:, :, :].rearrange("p f d -> p d f"), parts[:, :, 1, :],
                                  ALU.subtract).then_inc(low_ready, 1)

            def keep_embT(it, n, t):
                wait(dve, emb_turned, count(it, PAIR, t + 1))
                src = mid16[0:KP, 1, :].rearrange("p (d b) -> p b d", b=TB)
                dve.tensor_copy(embT[0:KP, n, :, D // 2:D], src).then_inc(embT_dve, 1)

            dve.memset(diag[:, :, :, :, :, :].bitcast(F32), 0.0).then_inc(ones_set, 1)
            dve.memset(erow[:, :, :, 0, F:J].bitcast(F32), 1.0).then_inc(ones_set, 1)
            dve.memset(erow[:, :, :, 1, F:J].bitcast(F32), 0.0).then_inc(ones_set, 1)
            dve.memset(pick[:, :, :], 0.0).then_inc(pair_step, 1)
            dve.memset(pairs[:, :, :, :], 0.0).then_inc(pair_step, 1)
            dve.wait_ge(pool_step, 7)
            dve.wait_ge(pair_step, 2)
            for r in range(R):
                for n in range(OPS):
                    dve.tensor_copy(pick[:, n, F * r:F * r + F], match[:, OFFSETS[r][n]:OFFSETS[r][n] + F]).then_inc(picks, 1)
            dve.wait_ge(w0_in, 16)
            dve.tensor_copy(raw0v[:, 0:F, F:WRAP], raw0v[:, 0:F, 0:WRAP - F]).then_inc(pair_step, 1)
            dve.wait_ge(pair_step, 3)
            dve.tensor_copy(raw0v[:, F:WRAP, :], raw0v[:, 0:WRAP - F, :]).then_inc(pair_step, 1)
            dve.wait_ge(pair_step, 4)
            for c, r, shift, a, b in runs():
                ab, ba = (raw0[:, x:x + (F - 1) * (WRAP + 1) + 1:WRAP + 1] for x in (a * WRAP + b, b * WRAP + a))
                if shift:
                    op = dve.tensor_tensor(pairs[:, c, r, :], ab, ba, ALU.add)
                else:
                    op = dve.tensor_copy(pairs[:, c, r, :], ab)
            op.then_inc(pairs_ready, 1)
            dve.wait_ge(kept_act, 1)
            dve.tensor_tensor(w0l[0:KP, :, :], mid[0:KP, :, :].rearrange("p a (c h) -> p (a c) h", h=H)[:, 0:CH, :],
                              w0h[0:KP, :, :].bitcast(F32), ALU.subtract).then_inc(kept_dve, 1)
            turns = 1
            for j in range(0, F, 8):
                n = min(8, F - j)
                turns += 1
                dve.wait_ge(turned, turns)
                dve.tensor_copy(w1T[:, j:j + n, :], mid[:, :, :].rearrange("p a (c h) -> p (a c) h", h=H)[:, 0:n, :]).then_inc(kept_dve, 1)
            for t in range(0, TILES, 8):
                turns += 1
                dve.wait_ge(turned, turns)
                dve.tensor_copy(denseT[:, t * TB:(t + 8) * TB], mid[0:K0, :, :].rearrange("p a b -> p (a b)")).then_inc(kept_dve, 1)
            split_rest(0, 0, 0)
            split_low(0, 0, 0)
            keep_embT(0, 0, 0)

            def slot(it, q):
                PB = PAIR * BLOCKS
                there, k = stage(it, q, 0)
                e0 = 2 * (q % 2)

                def multiply(e):
                    n = ENTRIES * k + e
                    wait(dve, picked, count(it, ENTRIES * PB, n + 1))
                    if e == 0:
                        wait(dve, opA_ready, count(it, PB, k + 1))
                        dve.tensor_tensor(ring[0][0:KP, 1, :], ring[0][0:KP, 1, :], opA[0:KP, k % 2, 0, :],
                                          ALU.mult).then_inc(product, 1)
                    else:
                        dve.tensor_tensor(ring[e % 2][0:KP, :, :], ring[e % 2][0:KP, 1:2, :].broadcast_to([KP, 2, COLS]),
                                          opA[0:KP, k % 2, :, :], ALU.mult).then_inc(product, 1)

                def low(e):
                    n = ENTRIES * k + e
                    wait(dve, hi_ready, count(it, ENTRIES * PB, n + 1))
                    wait(dve, layer0, count(it, ENTRIES * PB, n - ENTRIES + 1))
                    a = 1 if e == 0 else 0
                    dve.tensor_tensor(lo[0:KP, e, a:2, :], ring[e % 2][0:KP, a:2, :],
                                      hi[0:KP, e, a:2, :].bitcast(F32), ALU.subtract).then_inc(lo_ready, 1)

                if there:
                    multiply(e0)
                    multiply(e0 + 1)
                turn, t = ahead(it, q, SLOTS - 2, SLOTS - 1)
                if turn and q % SLOTS == SLOTS - 2:
                    keep_embT(it, t % 2, t)
                split, t = ahead(it, q, SPLIT, SLOTS - 1)
                if split:
                    split_rest(it, t % 2, t)
                if there:
                    low(e0)
                split, t = ahead(it, q, SPLIT + 1, SLOTS - 1)
                if split:
                    split_low(it, t % 2, t)
                if there:
                    low(e0 + 1)
                done, kx = stage(it, q, 3)
                if q % 2 and done:
                    wait(dve, erow_hi, count(it, PB, kx + 1))
                    dve.tensor_tensor(erow[:, kx % 2, :, 1, 0:F], mid[:, 1, 0:GROUPS * J].rearrange("p (g j) -> p g j", j=J)[:, :, 0:F],
                                      erow[:, kx % 2, :, 0, 0:F].bitcast(F32), ALU.subtract).then_inc(erow_lo, 1)
                    wait(dve, xTh_ready, count(it, PB, kx + 1))
                    dve.tensor_tensor(xTl[:, kx % 2, :, :], mid[:, 0, :].rearrange("p (g h) -> p g h", h=H),
                                      xTh[:, kx % 2, :, :].bitcast(F32), ALU.subtract).then_inc(xTl_ready, 1)
                turn, t = ahead(it, q, SLOTS - 2, SLOTS - 1)
                if turn and q % SLOTS == SLOTS - 1:
                    keep_embT(it, t % 2, t)

            slots(dve, slot)

        @block.tensor
        def _(pe):
            def turn_embedding(it, n, t):
                for d in range(D):
                    if d == 0:
                        wait(pe, low_ready, count(it, PAIR, t + 1))
                    op = pe.transpose(mid16[0:KP, d // 8, (d % 8) * TB:(d % 8 + 1) * TB],
                                      parts[:, d, :, :].rearrange("p a f -> p (a f)"), id16[:, :])
                op.then_inc(emb_turned, 1)

            pe.wait_ge(consts, 2)
            pe.wait_ge(pairs_ready, 1)
            for c in range(CH):
                op = pe.transpose(mid[0:KP, c // 4, (c % 4) * H:(c % 4 + 1) * H],
                                  pairs[:, c, :, :].rearrange("p r i -> p (r i)"), id32[:, :])
            op.then_inc(turned, 1)
            pe.wait_ge(w1_in, 16)
            for n, j0 in enumerate(range(0, F, 8)):
                pe.wait_ge(kept_dve, n + 1)
                for j in range(j0, min(j0 + 8, F)):
                    c = j - j0
                    op = pe.transpose(mid[:, c // 4, (c % 4) * H:(c % 4 + 1) * H], raw1[:, j:j + (H - 1) * F + 1:F], id32[:, :])
                op.then_inc(turned, 1)
            pe.wait_ge(dense_in, 16)
            for m, t0 in enumerate(range(0, TILES, 8)):
                pe.wait_ge(kept_dve, n + 2 + m)
                for c in range(8):
                    op = pe.transpose(mid[0:K0, c // 4, (c % 4) * TB:(c % 4 + 1) * TB], dense[:, t0 + c, :], id32[:, :])
                op.then_inc(turned, 1)
            pe.wait_ge(kept_dve, n + 3 + m)
            turn_embedding(0, 0, 0)
            pe.wait_ge(picks, R * OPS)
            pe.wait_ge(mlp_in, 16 * 6)

            def slot(it, q):
                PB = PAIR * BLOCKS

                def choose(k, e):
                    n = ENTRIES * k + e
                    if k % BLOCKS == 0 and e == 0:
                        wait(pe, embT_act, count(it, PAIR, k // BLOCKS + 1))
                        wait(pe, embT_dve, count(it, PAIR, k // BLOCKS + 1))
                    wait(pe, lo_ready, count(it, ENTRIES * PB, n - 1))
                    b0 = (k % BLOCKS) * BB
                    cols = embT[0:KP, (k // BLOCKS) % 2, b0:b0 + BB, :].rearrange("p b d -> p (b d)")
                    for a in range(2) if e == 0 else (1,):
                        op = pe.matmul(ring[e % 2][:, a, :], pick[:, e + a, :], cols, start=True, stop=True)
                    op.then_inc(picked, 1)

                def convolve(k, e):
                    n = ENTRIES * k + e
                    if e == 0:
                        wait(pe, x1_ready, count(it, PB, k))
                    chunks = [(a, 2 * e + a - 1) for a in range(2) if 2 * e + a]
                    wait(pe, hi_ready, count(it, ENTRIES * PB, n + 1))
                    for a, c in chunks:
                        pe.matmul(px[:, :], w0h[0:KP, c, :], hi[0:KP, e, a, :], start=(c == 0), stop=False)
                        pe.matmul(px[:, :], w0l[0:KP, c, :], hi[0:KP, e, a, :], start=False, stop=False)
                    wait(pe, lo_ready, count(it, ENTRIES * PB, n + 1))
                    for a, c in chunks:
                        op = pe.matmul(px[:, :], w0h[0:KP, c, :], lo[0:KP, e, a, :], start=False, stop=(c == CH - 1))
                    op.then_inc(layer0, 1)

                def correlate(kg, half):
                    for a in range(2):
                        g = 2 * half + a
                        terms = ((xTh, 0), (xTl, 0), (xTh, 1))
                        for m, (x, part) in enumerate(terms):
                            op = pe.matmul(mid[:, a, 0:GB * J], x[:, kg % 2, g, :], diag[:, kg % 2, g, :, part, :],
                                           start=(m == 0), stop=(m == len(terms) - 1))
                    op.then_inc(gram_done, 1)

                def second(t, part):
                    if part == 0:
                        wait(pe, gram_kept, count(it, 2 * PB, 2 * BLOCKS * (t + 1)))
                        wait(pe, y_ready, count(it, PAIR, t))
                    for j in range(part * OUT1_J, min(F, (part + 1) * OUT1_J)):
                        op = pe.matmul(acc[:, 0:TB], w1T[:, j, :], gram[:, t % 2, j, :], start=(j == 0), stop=(j == F - 1))
                    if part == OUT1_STEPS - 1:
                        op.then_inc(out1_done, 1)

                there, k = stage(it, q, 0)
                last, kl = stage(it, q, 1)
                e0 = 2 * (q % 2)
                el = 2 - e0
                if there:
                    choose(k, e0)
                gb, kg = stage(it, q, 7)
                if q % 2 and gb:
                    wait(pe, gram_kept, count(it, 2 * PB, 2 * kg + 1))
                    correlate(kg, 1)
                    if there:
                        choose(k, e0 + 1)
                    if last:
                        convolve(kl, el)
                else:
                    if last:
                        convolve(kl, el)
                    if there:
                        choose(k, e0 + 1)
                turn, t = ahead(it, q, SLOTS - 2, SLOTS - 1)
                if turn and q % SLOTS == SLOTS - 2:
                    _, kx = stage(it, q, 4)
                    wait(pe, xTl_ready, count(it, PB, kx + 1))
                    turn_embedding(it, t % 2, t)
                if last:
                    convolve(kl, el + 1)
                ga, kg = stage(it, q, 6)
                if q % 2 == 0 and ga:
                    wait(pe, diag_in[kg % 2], count(it, 16 * GB * PB // 2, 16 * GB * (kg // 2 + 1)))
                    after = 0 if isinstance(it, int) and it * PB + kg + 1 == TILES * BLOCKS else 1
                    wait(pe, xTh_ready, count(it, PB, kg + 1 + after))
                    wait(pe, xTl_ready, count(it, PB, kg + 1 + after))
                    if not after:
                        wait(pe, gram_kept, count(it, 2 * PB, 2 * kg))
                    if q % SLOTS in (0, SLOTS - 2):
                        last_t = (q + 2) // SLOTS
                        if isinstance(it, int):
                            late = it * PAIR + last_t <= PAIR and q % SLOTS == SLOTS - 2
                            last_t = min(last_t - late, TILES - PAIR * it - 1)
                        wait(pe, embT_act, count(it, PAIR, last_t + 1))
                        wait(pe, embT_dve, count(it, PAIR, last_t + 1))
                    correlate(kg, 0)
                done, kx = stage(it, q, 3)
                if q % 2 and done:
                    wait(pe, x1_ready, count(it, PB, kx + 1))
                    wait(pe, gram_kept, count(it, 2 * PB, 2 * kx - 2))
                    b0 = (kx % BLOCKS) * BB
                    for g in range(GROUPS):
                        pe.transpose(mid[:, 0, g * H:(g + 1) * H], x1[:, kx % 2, g * P:(g + 1) * P], id32[:, :])
                    for g in range(GROUPS):
                        cols = embT[0:KP, (kx // BLOCKS) % 2, b0 + g * GB:b0 + (g + 1) * GB, :].rearrange("p b d -> p (b d)")
                        op = pe.matmul(mid[:, 1, g * J:g * J + F], cols, match[:, 0:F], start=True, stop=True)
                    op.then_inc(x1_turned, 1)

                if turn and q % SLOTS == SLOTS - 1:
                    wait(pe, xTl_ready, count(it, PB, kx + 1))
                    turn_embedding(it, t % 2, t)

                there, t = stage(it, q, 14, SLOTS)
                if (q - 14) % SLOTS < OUT1_STEPS and there:
                    second(t, (q - 14) % SLOTS)
                there, t = stage(it, q, 18, SLOTS)
                if q % SLOTS == 3 and there:
                    wait(pe, z1_ready, count(it, PAIR, t + 1))
                    at = slice((PAIR * it + t) * TB, (PAIR * it + t + 1) * TB) if isinstance(it, int) else \
                        bass.ds(it * (PAIR * TB) + t * TB, TB)
                    for m in range(N1 // P):
                        w = slice(m * P, (m + 1) * P)
                        o = acc[:, m * TB:(m + 1) * TB]
                        pe.matmul(o, wt1[:, 0, w], gram[:, t % 2, F, :], start=True, stop=False)
                        pe.matmul(o, wt1[:, 1, w], z1[:, :], start=False, stop=False)
                        op = pe.matmul(o, wt1d[:, w], denseT[:, at], start=False, stop=True)
                    op.then_inc(l1_done, 1)
                if q % SLOTS == 4 and there:
                    wait(pe, h1_ready, count(it, PAIR, t + 1))
                    for m in range(N2 // P):
                        for c in range(N1 // P):
                            op = pe.matmul(acc[:, m * TB:(m + 1) * TB], wt2[:, c, m * P:(m + 1) * P], h1[:, c, :],
                                           start=(c == 0), stop=(c == N1 // P - 1))
                    op.then_inc(l2_done, 1)
                if q % SLOTS == 5 and there:
                    wait(pe, h2_ready, count(it, PAIR, t + 1))
                    for c in range(N2 // P):
                        op = pe.matmul(acc[0:1, 0:TB], wt3[:, c:c + 1], h2[:, c, :], start=(c == 0), stop=(c == N2 // P - 1))
                    op.then_inc(l3_done, 1)

            slots(pe, slot)


def kernel(**inputs):
    import numpy as _np
    import concourse.bacc as _bacc
    from concourse.bass_utils import run_bass_kernel_spmd as _run

    nc = _bacc.Bacc("TRN2", target_bir_lowering=False, num_devices=1)
    arrays, dram = {}, {}
    names = ["dense_ctx", "ids"] + TABLES + ["W_top1", "b_top1", "W_top2", "b_top2", "W_top3", "L0_rec_W0", "L0_rec_W1"]
    for name in names:
        a = _np.ascontiguousarray(inputs[name])
        arrays[f"in_{name}"] = a
        dram[name] = nc.dram_tensor(f"in_{name}", a.shape, mybir.dt.from_np(a.dtype), kind="ExternalInput").ap()
    y = nc.dram_tensor("out_y", (B, 1), F32, kind="ExternalOutput").ap()
    build(nc, dram["dense_ctx"], dram["ids"], [dram[n] for n in TABLES], dram["W_top1"], dram["b_top1"],
          dram["W_top2"], dram["b_top2"], dram["W_top3"], dram["L0_rec_W0"], dram["L0_rec_W1"], y)
    r = _run(nc, [arrays], core_ids=[0])
    return r.results[0]["out_y"]
```

```python
from contextlib import ExitStack

import concourse.bass as bass
from concourse import mybir

ALU = mybir.AluOpType
ACT = mybir.ActivationFunctionType
F32 = mybir.dt.float32
F32R = mybir.dt.float32r
BF16 = mybir.dt.bfloat16
I32 = mybir.dt.int32

B, F, D, H = 2048, 39, 16, 128
K0, N1, N2 = 16, 512, 256
P = 128
TB = P
TILES = B // TB
COLS = 512
BB = COLS // D
BLOCKS = TB // BB
GB = P // D
GROUPS = BB // GB
SHIFTS = (F + 1) // 2
OFFSETS = ((0, 2, 0, 3, 6), (0, 5, 14, 16, 18), (0, 7, 15, 17, 19))
R = len(OFFSETS)
KP = R * F
OPS = len(OFFSETS[0])
ENTRIES = OPS - 1
CHUNKS = [(0, 1)] + [(m, n) for n in range(2, OPS) for m in range(2)]
CH = len(CHUNKS)
WRAP = F + max(map(max, OFFSETS))
J = F + 1
TABLES = [f"tbl_{f}" for f in range(F)]
SLOTS = 2 * BLOCKS
PAIR = 2
S_IT = PAIR * SLOTS
SPLIT, TURN = 4, 6
SPLIT_LATE, TURN_LATE = (7, 6), (7, 7)
TAIL = 15
ITERS = TILES // PAIR
OUT1 = [(15 + i, 0, 6 * i, min(F, 6 * i + 6)) for i in range(7)] + \
       [(22 + i, 1, 8 * i, min(F, 8 * i + 8)) for i in range(5)]
TAIL_OUT1 = [(16, 0, 6, 11), (17, 0, 11, 20), (18, 0, 20, 25), (19, 0, 25, 31), (20, 0, 31, 35), (21, 0, 35, F)] + OUT1[7:]
L1_LAG, L2_LAG, L3_LAG = 27, 29, 30
DR = (0, 32, 64)
KD = DR[2] + K0
C = 8
assert ENTRIES == 4 and F % 2 == 1


def runs():
    seen = {}
    for c, (m, n) in enumerate(CHUNKS):
        for r in range(R):
            a, b = OFFSETS[r][m], OFFSETS[r][n]
            seen.setdefault(min((a - b) % F, (b - a) % F), (c, r, a, b))
    assert sorted(seen) == list(range(SHIFTS))
    return [(c, r, shift, a, b) for shift, (c, r, a, b) in seen.items()]


def count(it, per, local):
    return it * per + local


def wait(eng, sem, value):
    if not isinstance(value, int) or value > 0:
        eng.wait_ge(sem, value)


def tail(it):
    return isinstance(it, int) and it == ITERS


def slots(eng, emit):
    for q in range(S_IT):
        emit(0, q)
    with eng.Fori(1, ITERS - 1, 1) as it:
        for q in range(S_IT):
            emit(it, q)
    for it in (ITERS - 1, ITERS):
        for q in range(S_IT if it < ITERS else TAIL):
            emit(it, q)


def stage(it, q, lag, every=2):
    local = (q - lag) // every
    if isinstance(it, int):
        n = it * (S_IT // every) + local
        return 0 <= n < TILES * SLOTS // every, local
    return True, local


def ahead(it, q, at, late):
    there, t = stage(it, q, at - SLOTS, SLOTS)
    if isinstance(it, int) and 0 < it * PAIR + t <= len(late):
        at = late[it * PAIR + t - 1]
    return there and q % SLOTS == at, t


def build(nc, dense_ctx, ids, tables, W_top1, b_top1, W_top2, b_top2, W_top3, W0, W1, out):
    ROWS2 = PAIR * TB
    small = [f for f in range(F) if tables[f].shape[0] % C == 0 and tables[f].shape[0] // C <= P]
    S = len(small)
    GS = COLS // P
    groups = [small[g:g + GS] for g in range(0, S, GS)]
    KT = max([tables[f].shape[0] // C for f in small] + [1])
    assert len(groups) <= 4 and all(tables[f].shape[0] == KT * C for f in small)
    with ExitStack() as ctx:
        def sb(name, shape, dt=F32):
            return ctx.enter_context(nc.sbuf_tensor(name, shape, dt))

        def ps(name, shape):
            return ctx.enter_context(nc.psum_tensor(name, shape, F32))

        def sem(name):
            return ctx.enter_context(nc.semaphore(name))

        idx = sb("idx", [P, 2, F], I32)
        emb = sb("emb", [P, 2, F, D])
        rest = sb("rest", [P, F, D])
        parts = sb("parts", [P, D, 3, F], BF16)
        embT = sb("embT", [P, 2, TB, D], BF16)
        opA = sb("opA", [P, 2, 2, COLS])
        hi = sb("hi", [P, ENTRIES, 2, COLS], F32R)
        lo = sb("lo", [P, ENTRIES, 2, COLS], F32R)
        x1 = sb("x1", [P, 2, COLS])
        xTh = sb("xTh", [P, 2, GROUPS, H], F32R)
        xTl = sb("xTl", [P, 2, GROUPS, H], F32R)
        erow = sb("erow", [P, 2, GROUPS, 2, J], F32R)
        diag = sb("diag", [P, 2, GROUPS, GB, 2, J], F32R)
        gram = sb("gram", [P, 2, J, TB])
        w0h = sb("w0h", [P, CH, H], F32R)
        w0l = sb("w0l", [P, CH, H], F32R)
        w1T = sb("w1T", [P, F, H])
        wt1h = sb("wt1h", [P, 2, N1], F32R)
        wt1l = sb("wt1l", [P, 2, N1], F32R)
        wt1d = sb("wt1d", [KD, N1], F32R)
        wt2h = sb("wt2h", [P, N1 // P, N2], F32R)
        wt2l = sb("wt2l", [P, N1 // P, N2], F32R)
        wt3 = sb("wt3", [P, N2 // P])
        bt1 = sb("bt1", [P, N1 // P])
        bt2 = sb("bt2", [P, N2 // P])
        denseT = sb("denseT", [KD, B], F32R)
        o0h = sb("o0h", [P, PAIR, TB], F32R)
        o0l = sb("o0l", [P, PAIR, TB], F32R)
        z1h = sb("z1h", [P, PAIR, TB], F32R)
        z1l = sb("z1l", [P, PAIR, TB], F32R)
        h1h = sb("h1h", [P, N1 // P, ROWS2], F32R)
        h1l = sb("h1l", [P, N1 // P, ROWS2], F32R)
        h2 = sb("h2", [P, N2 // P, ROWS2])
        y = sb("y", [1, ROWS2])
        id32 = sb("id32", [P, P])
        id16 = sb("id16", [P, P], BF16)
        match = sb("match", [KP, WRAP], BF16)
        pick = sb("pick", [KP, OPS, P], BF16)

        ring = [ps(f"ring{n}", [P, 2, COLS]) for n in range(2)]
        px = ps("px", [P, COLS])
        acc = ps("acc", [P, COLS])
        mid = ps("mid", [P, 2, COLS])
        def bank(it, second):
            return px if second and tail(it) else acc

        mid16 = mid[:, :, :].bitcast(BF16)

        gflat = gram[:, :, :, :].rearrange("p a j b -> p (a j b)")
        raw1 = gflat[:, 0:H * F]
        raw0 = gflat[:, J * TB:J * TB + WRAP * WRAP]
        raw0v = raw0.rearrange("p (i j) -> p i j", j=WRAP)
        n0 = J * TB + WRAP * WRAP
        pairs = gflat[:, n0:n0 + CH * KP].rearrange("p (c r i) -> p c r i", r=R, i=F)
        aflat = opA[:, :, :, :].rearrange("p n a c -> p (n a c)")
        wt1 = aflat[:, 0:2 * N1].rearrange("p (c n) -> p c n", n=N1)
        wt1d_raw = aflat[0:KD, 2 * N1:3 * N1]
        wt2 = x1[:, :, :].rearrange("p a c -> p (a c)").rearrange("p (c n) -> p c n", n=N2)
        dense = embT[:, :, :, :].bitcast(F32).rearrange("p n b d -> p (n b d)")[:, 0:TILES * KD].rearrange("p (t k) -> p t k", k=KD)

        tabs = w1T[0:KT, F - S:F, :]
        onehot = lo[0:KT, :, :, :].rearrange("p e a c -> p (e a c)")[:, 0:S * P]
        rflat = rest[:, :, :].rearrange("p f d -> p (f d)")
        look = rflat[:, 0:2 * F].rearrange("p (a f) -> p a f", f=F)
        look_i = rflat[:, 2 * F:4 * F].bitcast(I32).rearrange("p (a f) -> p a f", f=F)
        numb = rflat[:, 4 * F:4 * F + C + 1]
        numb_i = rflat[:, 4 * F + C + 1:4 * F + 2 * (C + 1)].bitcast(I32)
        mask = rflat[:, 5 * F:5 * F + F * C].rearrange("p (f c) -> p f c", c=C)

        ids_in = [sem(f"ids_in{n}") for n in range(2)]
        gathered = [sem(f"gathered{n}") for n in range(2)]
        w0_in, w1_in, dense_in, mlp_in = sem("w0_in"), sem("w1_in"), sem("dense_in"), sem("mlp_in")
        consts, picks, ones_set = sem("consts"), sem("picks"), sem("ones_set")
        gather_open = sem("gather_open")
        pool_step = sem("pool_step")
        pairs_ready, pair_step = sem("pairs_ready"), sem("pair_step")
        turned = sem("turned")
        kept_act, kept_dve = sem("kept_act"), sem("kept_dve")
        top_ready, rest_ready, mid_ready, low_ready = sem("top_ready"), sem("rest_ready"), sem("mid_ready"), sem("low_ready")
        emb_turned, embT_act, embT_dve = sem("emb_turned"), sem("embT_act"), sem("embT_dve")
        picked, opA_ready, product, hi_ready, lo_ready = sem("picked"), sem("opA_ready"), sem("product"), sem("hi_ready"), sem("lo_ready")
        layer0, x1_ready, x1_turned = sem("layer0"), sem("x1_ready"), sem("x1_turned")
        xTh_ready, xTl_ready, erow_hi, erow_lo = sem("xTh_ready"), sem("xTl_ready"), sem("erow_hi"), sem("erow_lo")
        diag_in = [sem(f"diag_in{n}") for n in range(2)]
        gram_done, gram_kept = sem("gram_done"), sem("gram_kept")
        cleared, mlp_high, mlp_low = sem("cleared"), sem("mlp_high"), sem("mlp_low")
        out0_hi, out0_lo = sem("out0_hi"), sem("out0_lo")
        out1_done, z1_hi, z1_lo = sem("out1_done"), sem("z1_hi"), sem("z1_lo")
        l1_done, h1_hi, h1_lo = sem("l1_done"), sem("h1_hi"), sem("h1_lo")
        l2_done, h2_ready, l3_done, y_ready = sem("l2_done"), sem("h2_ready"), sem("l3_done"), sem("y_ready")
        dense_hi, stored = sem("dense_hi"), sem("stored")
        turn_bank = (mid, ring[0], ring[1])
        W1_TURNS = [range(j, min(j + 8, F)) for j in range(0, F, 8)]
        DENSE_TURNS = [range(t, t + 8) for t in range(0, TILES, 8)]
        tabs_in, counted, look_step = sem("tabs_in"), sem("counted"), sem("look_step")
        spread, hot, looked, looked_up = sem("spread"), sem("hot"), sem("looked"), sem("looked_up")

        def landed(it, n, tile):
            return count(it, 16 * F, 16 * F * (tile // 2 + 1)) - (16 * S if n == 0 else 0)

        ids_t = ids.rearrange("(t p) f -> t p f", p=TB)
        out_t = out.rearrange("(t b) o -> t o b", b=ROWS2)

        block = ctx.enter_context(nc.Block())

        @block.sync
        def _(sp):
            def load_ids(it, n):
                wait(sp, gathered[n], landed(it, n, n - PAIR))
                src = ids_t[PAIR * it + n] if isinstance(it, int) else \
                    ids_t[bass.ds(PAIR * it + n, 1)].rearrange("a p f -> p (a f)")
                sp.dma_start(idx[:, n, :], src).then_inc(ids_in[n], 16)

            load_ids(0, 0)
            load_ids(0, 1)
            sp.dma_start(raw0v[:, 0:F, 0:F], W0.rearrange("h (i j) -> h i j", j=F)).then_inc(w0_in, 16)
            for k, f in enumerate(small):
                sp.dma_start(tabs[:, k, :], tables[f].rearrange("(p c) d -> p (c d)", c=C)).then_inc(tabs_in, 16)
            sp.dma_start(raw1, W1).then_inc(w1_in, 16)
            sp.wait_ge(cleared, 2)
            for r in DR:
                sp.dma_start(dense[:, :, r:r + K0], dense_ctx.rearrange("(t p) k -> p t k", p=TB)).then_inc(dense_in, 16)
            sp.dma_start(wt1[:, :, :], W_top1[0:2 * P, :].rearrange("(c p) n -> p c n", p=P)).then_inc(mlp_in, 16)
            for r in DR:
                sp.dma_start(wt1d_raw[r:r + K0, :], W_top1[2 * P:2 * P + K0, :]).then_inc(mlp_in, 16)
            sp.dma_start(wt2[:, :, :], W_top2.rearrange("(c p) n -> p c n", p=P)).then_inc(mlp_in, 16)
            sp.dma_start(wt3[:, :], W_top3.rearrange("(c p) n -> p (c n)", p=P), allow_slow_non_contiguous=True).then_inc(mlp_in, 16)
            sp.dma_start(bt1[:, :], b_top1.rearrange("(c p) -> p c", p=P), allow_slow_non_contiguous=True).then_inc(mlp_in, 16)
            sp.dma_start(bt2[:, :], b_top2.rearrange("(c p) -> p c", p=P), allow_slow_non_contiguous=True).then_inc(mlp_in, 16)

            def slot(it, q):
                there, k = stage(it, q, 3)
                if q % 2 and there:
                    if isinstance(it, int) and it == 0 and k == 0:
                        sp.wait_ge(ones_set, 3)
                    wait(sp, erow_hi, count(it, PAIR * BLOCKS, k + 1))
                    wait(sp, erow_lo, count(it, PAIR * BLOCKS, k + 1))
                    for b in range(GB):
                        at = slice(D * b, D * b + D)
                        sp.dma_start(diag[at, k % 2, :, b, :, :].rearrange("p g a j -> p g (a j)").bitcast(F32),
                                     erow[at, k % 2, :, :, :].rearrange("p g a j -> p g (a j)").bitcast(F32)).then_inc(diag_in[k % 2], 16)
                if q % SLOTS == 0:
                    n = q // SLOTS
                    if isinstance(it, int) and it == 0 and n == 0:
                        sp.wait_ge(looked_up, S)
                    if not isinstance(it, int):
                        load_ids(it + 1, n)
                    elif it + 1 < ITERS:
                        load_ids(it + 1, n)
                there, s = stage(it, q, L3_LAG, S_IT)
                if q == L3_LAG % S_IT and there:
                    wait(sp, y_ready, count(it, 1, s + 1))
                    dst = out_t[it + s] if isinstance(it, int) else \
                        out_t[bass.ds(it + s, 1)].rearrange("a o b -> (a o) b")
                    sp.dma_start(dst, y[:, :]).then_inc(stored, 16)

            slots(sp, slot)
            sp.wait_ge(stored, 16 * ITERS)

        @block.gpsimd
        def _(pool):
            pool.iota(numb_i[:, 0:C], [[1, C]], base=0, channel_multiplier=0).then_inc(counted, 1)
            pool.iota(numb_i[:, C:C + 1], [[0, 1]], base=0, channel_multiplier=1).then_inc(counted, 1)
            pool.memset(id32[:, :], 0.0).then_inc(pool_step, 1)
            pool.memset(id16[:, :], 0.0).then_inc(pool_step, 1)
            pool.memset(match[:, :], 0.0).then_inc(pool_step, 1)
            pool.wait_ge(pool_step, 3)
            for m in (id32, id16):
                pool.affine_select(out=m[:, :], in_=m[:, :], compare_op=ALU.not_equal, fill=1.0, base=0,
                                   pattern=[[-1, P]], channel_multiplier=1).then_inc(consts, 1)
            for n, m in enumerate((-1, 0, 1, 2)):
                pool.wait_ge(pool_step, 3 + n)
                pool.affine_select(out=match[:, :], in_=match[:, :], compare_op=ALU.not_equal, fill=1.0,
                                   base=-F * m, pattern=[[-1, WRAP]],
                                   channel_multiplier=1).then_inc(pool_step, 1)
            pool.wait_ge(pool_step, 7)

            def gather(it, n):
                wait(pool, low_ready, count(it, PAIR, n - 1))
                wait(pool, ids_in[n], count(it, 16, 16))
                pool.sem_inc(gather_open, 1)
                first = isinstance(it, int) and it == 0 and n == 0
                for f in [f for f in range(F) if not (first and f in small)]:
                    pool.indirect_dma_start(
                        out=emb[:, n, f, :], out_offset=None, in_=tables[f],
                        in_offset=bass.IndirectOffsetOnAxis(ap=idx[:, n, f:f + 1], axis=0),
                    ).then_inc(gathered[n], 16)

            for n in range(PAIR):
                gather(0, n)
            with pool.Fori(1, ITERS, 1) as it:
                for n in range(PAIR):
                    gather(it, n)

        @block.scalar
        def _(act):
            def copy(dst, src):
                return act.activation(dst, src, ACT.Copy)

            def split_top(it, n, t):
                wait(act, gathered[n], landed(it, n, t))
                if isinstance(it, int) and it * PAIR + t == 0:
                    act.wait_ge(looked_up, S)
                wait(act, emb_turned, count(it, PAIR, t))
                copy(parts[:, :, 0, :], emb[:, n, :, :].rearrange("p f d -> p d f")).then_inc(top_ready, 1)

            def split_mid(it, n, t):
                wait(act, rest_ready, count(it, PAIR, t + 1))
                copy(parts[:, :, 1, :], rest[:, :, :].rearrange("p f d -> p d f")).then_inc(mid_ready, 1)

            def keep_embT(it, n, t):
                wait(act, emb_turned, count(it, PAIR, t + 1))
                src = mid16[0:KP, 0, :].rearrange("p (d b) -> p b d", b=TB)
                copy(embT[0:KP, n, :, 0:D // 2], src).then_inc(embT_act, 1)

            act.wait_ge(consts, 1)
            act.activation(diag[:, :, :, :, :, :].rearrange("p n g b a j -> p (n g b a j)"),
                           id32[:, 0:1].broadcast_to([P, 2 * GROUPS * GB * 2 * J]), ACT.Copy, scale=0.0).then_inc(ones_set, 1)
            act.wait_ge(turned, 1)
            copy(w0h[0:KP, :, :], mid[0:KP, :, :].rearrange("p a (c h) -> p (a c) h", h=H)[:, 0:CH, :]).then_inc(kept_act, 1)
            for n, js in enumerate(W1_TURNS):
                if n == 1:
                    act.wait_ge(mlp_in, 16 * 8)
                    for raw, high_part in ((wt1d_raw, wt1d[:, :]), (wt1, wt1h[:, :, :]), (wt2, wt2h[:, :, :])):
                        copy(high_part, raw).then_inc(mlp_high, 1)
                if n == 1:
                    continue
                act.wait_ge(turned, n + 2)
                src = turn_bank[(n + 1) % 3][:, :, :].rearrange("p a (c h) -> p (a c) h", h=H)
                copy(w1T[:, js[0]:js[-1] + 1, :], src[:, 0:len(js), :]).then_inc(kept_act, 1)
            for n, ts in enumerate(DENSE_TURNS):
                turn = 1 + len(W1_TURNS) + n
                act.wait_ge(turned, turn + 1)
                copy(denseT[:, ts[0] * TB:(ts[-1] + 1) * TB],
                     turn_bank[turn % 3][0:KD, :, :].rearrange("p a b -> p (a b)")).then_inc(dense_hi, 1)
            split_top(0, 0, 0)
            split_mid(0, 0, 0)
            keep_embT(0, 0, 0)

            def slot(it, q):
                there, k = stage(it, q, 0)
                PB = PAIR * BLOCKS
                e0 = 2 * (q % 2)
                r = ENTRIES * k + e0
                if there and q % 2 == 0:
                    wait(act, picked, count(it, ENTRIES * PB, r + 1))
                    wait(act, product, count(it, ENTRIES * PB, ENTRIES * (k - 1)))
                    copy(opA[0:KP, k % 2, :, :], ring[0][0:KP, :, :]).then_inc(opA_ready, 1)

                def high(e):
                    n = ENTRIES * k + e
                    wait(act, product, count(it, ENTRIES * PB, n + 1))
                    wait(act, layer0, count(it, ENTRIES * PB, n - ENTRIES + 1))
                    a = 1 if e == 0 else 0
                    copy(hi[0:KP, e, a:2, :], ring[e % 2][0:KP, a:2, :]).then_inc(hi_ready, 1)

                def keep_gram(kg, half):
                    n = 2 * kg + half
                    wait(act, gram_done, count(it, 2 * PB, n + 1))
                    if kg % BLOCKS == 0 and half == 0:
                        wait(act, out1_done, count(it, PAIR, kg // BLOCKS - 1))
                        wait(act, out0_lo, count(it, PAIR, kg // BLOCKS - 1))
                    b0 = (kg % BLOCKS) * BB + half * 2 * GB
                    src = mid[:, :, 0:GB * J].rearrange("p a (b j) -> p j a b", j=J)
                    dst = gram[:, (kg // BLOCKS) % 2, :, b0:b0 + 2 * GB].rearrange("p j (a b) -> p j a b", a=2)
                    copy(dst, src).then_inc(gram_kept, 1)

                gb, kg = stage(it, q, 7)
                if q % 2 and gb:
                    keep_gram(kg, 1)
                split, t = ahead(it, q, SPLIT, SPLIT_LATE)
                if split:
                    split_top(it, t % 2, t)
                turn, t = ahead(it, q, TURN, TURN_LATE)
                if turn and q % SLOTS == TURN:
                    keep_embT(it, t % 2, t)
                if there:
                    high(e0)
                split, t = ahead(it, q, SPLIT, SPLIT_LATE)
                if split and q % 2:
                    split_mid(it, t % 2, t)
                if there:
                    high(e0 + 1)
                ga, kg = stage(it, q, 6)
                if q % 2 == 0 and ga:
                    keep_gram(kg, 0)
                split, t = ahead(it, q, SPLIT, SPLIT_LATE)
                if split and q % 2 == 0:
                    split_mid(it, t % 2, t)
                done, kx = stage(it, q, 2)
                if q % 2 == 0 and done:
                    wait(act, layer0, count(it, ENTRIES * PB, ENTRIES * (kx + 1)))
                    wait(act, x1_turned, count(it, PB, kx - 1))
                    copy(x1[:, kx % 2, :], px[:, :]).then_inc(x1_ready, 1)
                turn, t = ahead(it, q, TURN, TURN_LATE)
                if turn and q % SLOTS != TURN:
                    keep_embT(it, t % 2, t)
                done, kx = stage(it, q, 3)
                if q % 2 and done:
                    wait(act, x1_turned, count(it, PB, kx + 1))
                    wait(act, diag_in[kx % 2], count(it, 16 * GB * PB // 2, 16 * GB * (kx // 2)))
                    copy(erow[:, kx % 2, :, 0, 0:F], mid[:, 1, 0:GROUPS * J].rearrange("p (g j) -> p g j", j=J)[:, :, 0:F]).then_inc(erow_hi, 1)
                    copy(xTh[:, kx % 2, :, :], mid[:, 0, :].rearrange("p (g h) -> p g h", h=H)).then_inc(xTh_ready, 1)

                for n, lag in enumerate((14, 22)):
                    there, s = stage(it, q, lag, S_IT)
                    if q == lag % S_IT and there:
                        t = PAIR * s + n
                        wait(act, gram_kept, count(it, 2 * PAIR * BLOCKS, 2 * BLOCKS * (t + 1)))
                        copy(o0h[:, n, :], gram[:, n, F, :]).then_inc(out0_hi, 1)
                for n, lag in enumerate((21, 26)):
                    there, s = stage(it, q, lag, S_IT)
                    if q == lag % S_IT and there:
                        wait(act, out1_done, count(it, PAIR, PAIR * s + n + 1))
                        copy(z1h[:, n, :], bank(it, n)[:, 0:TB]).then_inc(z1_hi, 1)
                for half in range(2):
                    there, s = stage(it, q, L1_LAG + half, S_IT)
                    if q == (L1_LAG + half) % S_IT and there:
                        wait(act, l1_done, count(it, 2, 2 * s + half + 1))
                        for a in range(2):
                            m = 2 * half + a
                            at = bank(it, half)[:, a * ROWS2:(a + 1) * ROWS2]
                            act.activation(h1h[:, m, :], at, ACT.Relu, bias=bt1[:, m:m + 1])
                            op = act.activation(at, at, ACT.Relu, bias=bt1[:, m:m + 1])
                        op.then_inc(h1_hi, 1)
                there, s = stage(it, q, L2_LAG, S_IT)
                if q == L2_LAG % S_IT and there:
                    wait(act, l2_done, count(it, 1, s + 1))
                    for m in range(N2 // P):
                        op = act.activation(h2[:, m, :], acc[:, m * ROWS2:(m + 1) * ROWS2], ACT.Relu, bias=bt2[:, m:m + 1])
                    op.then_inc(h2_ready, 1)
                there, s = stage(it, q, L3_LAG, S_IT)
                if q == L3_LAG % S_IT and there:
                    wait(act, l3_done, count(it, 1, s + 1))
                    wait(act, stored, count(it, 16, 16 * s))
                    copy(y[:, :], acc[0:1, 0:ROWS2]).then_inc(y_ready, 1)

            slots(act, slot)

        @block.vector
        def _(dve):
            def split_rest(it, n, t):
                wait(dve, top_ready, count(it, PAIR, t + 1))
                dve.tensor_tensor(rest[:, :, :], emb[:, n, :, :], parts[:, :, 0, :].rearrange("p d f -> p f d"),
                                  ALU.subtract).then_inc(rest_ready, 1)

            def split_low(it, n, t):
                wait(dve, mid_ready, count(it, PAIR, t + 1))
                dve.tensor_tensor(parts[:, :, 2, :], rest[:, :, :].rearrange("p f d -> p d f"), parts[:, :, 1, :],
                                  ALU.subtract).then_inc(low_ready, 1)

            def keep_embT(it, n, t):
                wait(dve, emb_turned, count(it, PAIR, t + 1))
                src = mid16[0:KP, 1, :].rearrange("p (d b) -> p b d", b=TB)
                dve.tensor_copy(embT[0:KP, n, :, D // 2:D], src).then_inc(embT_dve, 1)

            dve.memset(dense[:, :, :], 0.0).then_inc(cleared, 1)
            dve.memset(wt1d_raw, 0.0).then_inc(cleared, 1)
            dve.wait_ge(counted, 2)
            dve.tensor_copy(numb, numb_i).then_inc(look_step, 1)
            dve.wait_ge(ids_in[0], 16)
            dve.tensor_scalar(look_i[:, 0, :], idx[:, 0, :], C.bit_length() - 1, None, ALU.logical_shift_right).then_inc(look_step, 1)
            dve.tensor_scalar(look_i[:, 1, :], idx[:, 0, :], C - 1, None, ALU.bitwise_and).then_inc(look_step, 1)
            dve.wait_ge(look_step, 3)
            dve.tensor_copy(look[:, :, :], look_i[:, :, :]).then_inc(look_step, 1)
            dve.wait_ge(look_step, 4)
            dve.tensor_tensor(mask[:, :, :], look[:, 1, :].unsqueeze(2).broadcast_to([P, F, C]),
                              numb[:, 0:C].unsqueeze(1).broadcast_to([P, F, C]), ALU.is_equal).then_inc(look_step, 1)
            for g, fields in enumerate(groups):
                dve.wait_ge(spread, g + 1)
                n = len(fields) * P
                dve.tensor_scalar(onehot[:, g * COLS:g * COLS + n], ring[g // 2][0:KT, g % 2, 0:n],
                                  numb[0:KT, C:C + 1], None, ALU.is_equal).then_inc(hot, 1)
            dve.memset(erow[:, :, :, 0, F:J].bitcast(F32), 1.0).then_inc(ones_set, 1)
            dve.memset(erow[:, :, :, 1, F:J].bitcast(F32), 0.0).then_inc(ones_set, 1)
            dve.memset(pick[:, :, :], 0.0).then_inc(pair_step, 1)
            dve.memset(pairs[:, :, :, :], 0.0).then_inc(pair_step, 1)
            dve.wait_ge(pool_step, 7)
            dve.wait_ge(pair_step, 2)
            for r in range(R):
                for n in range(OPS):
                    dve.tensor_copy(pick[:, n, F * r:F * r + F], match[:, OFFSETS[r][n]:OFFSETS[r][n] + F]).then_inc(picks, 1)
            dve.wait_ge(w0_in, 16)
            dve.tensor_copy(raw0v[:, 0:F, F:WRAP], raw0v[:, 0:F, 0:WRAP - F]).then_inc(pair_step, 1)
            dve.wait_ge(pair_step, 3)
            dve.tensor_copy(raw0v[:, F:WRAP, :], raw0v[:, 0:WRAP - F, :]).then_inc(pair_step, 1)
            dve.wait_ge(pair_step, 4)
            for c, r, shift, a, b in runs():
                ab, ba = (raw0[:, x:x + (F - 1) * (WRAP + 1) + 1:WRAP + 1] for x in (a * WRAP + b, b * WRAP + a))
                if shift:
                    op = dve.tensor_tensor(pairs[:, c, r, :], ab, ba, ALU.add)
                else:
                    op = dve.tensor_copy(pairs[:, c, r, :], ab)
            op.then_inc(pairs_ready, 1)
            dve.wait_ge(look_step, 5)
            for g, fields in enumerate(groups):
                if g == 2:
                    dve.wait_ge(kept_act, 1)
                    dve.tensor_tensor(w0l[0:KP, :, :], mid[0:KP, :, :].rearrange("p a (c h) -> p (a c) h", h=H)[:, 0:CH, :],
                                      w0h[0:KP, :, :].bitcast(F32), ALU.subtract).then_inc(kept_dve, 1)
                dve.wait_ge(looked, g + 1)
                rows = ring[g // 2][:, g % 2, 0:len(fields) * P].rearrange("p (f c d) -> p f c d", c=C, d=D)
                for k, f in enumerate(fields):
                    dve.tensor_tensor(rows[:, k, :, :], rows[:, k, :, :], mask[:, f, :].unsqueeze(2).broadcast_to([P, C, D]),
                                      ALU.mult).then_inc(look_step, 1)
                dve.wait_ge(look_step, 5 + sum(map(len, groups[:g + 1])))
                for k, f in enumerate(fields):
                    dve.tensor_reduce(emb[:, 0, f, :], rows[:, k, :, :].rearrange("p c d -> p d c"),
                                      mybir.AxisListType.X, ALU.add).then_inc(looked_up, 1)
            js = W1_TURNS[1]
            dve.wait_ge(turned, 3)
            dve.tensor_copy(w1T[:, js[0]:js[-1] + 1, :],
                            ring[1][:, :, :].rearrange("p a (c h) -> p (a c) h", h=H)[:, 0:len(js), :]).then_inc(kept_dve, 1)
            dve.wait_ge(mlp_high, 3)
            at = slice(DR[1], DR[1] + K0)
            dve.tensor_tensor(wt1d[at, :], wt1d_raw[at, :], wt1d[at, :].bitcast(F32), ALU.subtract).then_inc(mlp_low, 1)
            dve.tensor_tensor(wt1l[:, :, :], wt1, wt1h[:, :, :].bitcast(F32), ALU.subtract).then_inc(mlp_low, 1)
            dve.tensor_tensor(wt2l[:, :, :], wt2, wt2h[:, :, :].bitcast(F32), ALU.subtract).then_inc(mlp_low, 1)
            for n, ts in enumerate(DENSE_TURNS):
                turn = 1 + len(W1_TURNS) + n
                src = turn_bank[turn % 3][0:KD, :, :].rearrange("p a b -> p (a b)")
                cols = slice(ts[0] * TB, (ts[-1] + 1) * TB)
                dve.wait_ge(dense_hi, n + 1)
                dve.tensor_tensor(denseT[DR[2]:KD, cols], src[DR[2]:KD, :],
                                  denseT[DR[2]:KD, cols].bitcast(F32), ALU.subtract).then_inc(kept_dve, 1)
            split_rest(0, 0, 0)
            split_low(0, 0, 0)
            keep_embT(0, 0, 0)

            def slot(it, q):
                PB = PAIR * BLOCKS
                there, k = stage(it, q, 0)
                e0 = 2 * (q % 2)

                def multiply(e):
                    n = ENTRIES * k + e
                    wait(dve, picked, count(it, ENTRIES * PB, n + 1))
                    if e == 0:
                        wait(dve, opA_ready, count(it, PB, k + 1))
                        dve.tensor_tensor(ring[0][0:KP, 1, :], ring[0][0:KP, 1, :], opA[0:KP, k % 2, 0, :],
                                          ALU.mult).then_inc(product, 1)
                    else:
                        dve.tensor_tensor(ring[e % 2][0:KP, :, :], ring[e % 2][0:KP, 1:2, :].broadcast_to([KP, 2, COLS]),
                                          opA[0:KP, k % 2, :, :], ALU.mult).then_inc(product, 1)

                def low(e):
                    n = ENTRIES * k + e
                    wait(dve, hi_ready, count(it, ENTRIES * PB, n + 1))
                    wait(dve, layer0, count(it, ENTRIES * PB, n - ENTRIES + 1))
                    a = 1 if e == 0 else 0
                    dve.tensor_tensor(lo[0:KP, e, a:2, :], ring[e % 2][0:KP, a:2, :],
                                      hi[0:KP, e, a:2, :].bitcast(F32), ALU.subtract).then_inc(lo_ready, 1)

                if there:
                    multiply(e0)
                turn, t = ahead(it, q, TURN, TURN_LATE)
                if turn and q % SLOTS == TURN:
                    keep_embT(it, t % 2, t)
                if there:
                    multiply(e0 + 1)
                split, t = ahead(it, q, SPLIT, SPLIT_LATE)
                if split:
                    split_rest(it, t % 2, t)
                if there:
                    low(e0)
                split, t = ahead(it, q, SPLIT, SPLIT_LATE)
                if split and q % 2:
                    split_low(it, t % 2, t)
                if there:
                    low(e0 + 1)
                if split and q % 2 == 0:
                    split_low(it, t % 2, t)
                turn, t = ahead(it, q, TURN, TURN_LATE)
                if turn and q % SLOTS != TURN:
                    keep_embT(it, t % 2, t)
                done, kx = stage(it, q, 3)
                if q % 2 and done:
                    wait(dve, erow_hi, count(it, PB, kx + 1))
                    dve.tensor_tensor(erow[:, kx % 2, :, 1, 0:F], mid[:, 1, 0:GROUPS * J].rearrange("p (g j) -> p g j", j=J)[:, :, 0:F],
                                      erow[:, kx % 2, :, 0, 0:F].bitcast(F32), ALU.subtract).then_inc(erow_lo, 1)
                    wait(dve, xTh_ready, count(it, PB, kx + 1))
                    dve.tensor_tensor(xTl[:, kx % 2, :, :], mid[:, 0, :].rearrange("p (g h) -> p g h", h=H),
                                      xTh[:, kx % 2, :, :].bitcast(F32), ALU.subtract).then_inc(xTl_ready, 1)

                for n, lag in enumerate((14, 22)):
                    there, s = stage(it, q, lag, S_IT)
                    if q == lag % S_IT and there:
                        wait(dve, out0_hi, count(it, PAIR, PAIR * s + n + 1))
                        dve.tensor_tensor(o0l[:, n, :], gram[:, n, F, :], o0h[:, n, :].bitcast(F32),
                                          ALU.subtract).then_inc(out0_lo, 1)
                for n, lag in enumerate((21, 26)):
                    there, s = stage(it, q, lag, S_IT)
                    if q == lag % S_IT and there:
                        wait(dve, z1_hi, count(it, PAIR, PAIR * s + n + 1))
                        dve.tensor_tensor(z1l[:, n, :], bank(it, n)[:, 0:TB], z1h[:, n, :].bitcast(F32),
                                          ALU.subtract).then_inc(z1_lo, 1)
                for half in range(2):
                    there, s = stage(it, q, L1_LAG + half, S_IT)
                    if q == (L1_LAG + half) % S_IT and there:
                        wait(dve, h1_hi, count(it, 2, 2 * s + half + 1))
                        m = slice(2 * half, 2 * half + 2)
                        dve.tensor_tensor(h1l[:, m, :], bank(it, half)[:, :].rearrange("p (m b) -> p m b", b=ROWS2),
                                          h1h[:, m, :].bitcast(F32), ALU.subtract).then_inc(h1_lo, 1)

            slots(dve, slot)

        @block.tensor
        def _(pe):
            def turn_embedding(it, n, t):
                for d in range(D):
                    if d == 0:
                        wait(pe, low_ready, count(it, PAIR, t + 1))
                    op = pe.transpose(mid16[0:KP, d // 8, (d % 8) * TB:(d % 8 + 1) * TB],
                                      parts[:, d, :, :].rearrange("p a f -> p (a f)"), id16[:, :])
                op.then_inc(emb_turned, 1)

            pe.wait_ge(consts, 2)
            pe.wait_ge(look_step, 4)
            for g, fields in enumerate(groups):
                for k, f in enumerate(fields):
                    op = pe.matmul(ring[g // 2][0:KT, g % 2, k * P:(k + 1) * P], look[:, 0, f:f + 1].broadcast_to([P, KT]),
                                   id32[:, :], start=True, stop=True)
                op.then_inc(spread, 1)
            pe.wait_ge(tabs_in, 16 * S)
            for g, fields in enumerate(groups):
                pe.wait_ge(hot, g + 1)
                for k, f in enumerate(fields):
                    at = (g * GS + k) * P
                    op = pe.matmul(ring[g // 2][:, g % 2, k * P:(k + 1) * P], onehot[:, at:at + P].bitcast(F32),
                                   tabs[:, g * GS + k, :], start=True, stop=True)
                op.then_inc(looked, 1)
            pe.wait_ge(pairs_ready, 1)
            for c in range(CH):
                op = pe.transpose(mid[0:KP, c // 4, (c % 4) * H:(c % 4 + 1) * H],
                                  pairs[:, c, :, :].rearrange("p r i -> p (r i)"), id32[:, :])
            op.then_inc(turned, 1)
            pe.wait_ge(w1_in, 16)
            for n, js in enumerate(W1_TURNS):
                if n < 2:
                    pe.wait_ge(looked_up, min(S, 2 * GS * (n + 1)))
                elif n == 2:
                    pe.wait_ge(kept_dve, 1)
                elif n == 3:
                    pe.wait_ge(kept_act, 2)
                else:
                    pe.wait_ge(kept_dve, 2)
                for c, j in enumerate(js):
                    op = pe.transpose(turn_bank[(n + 1) % 3][:, c // 4, (c % 4) * H:(c % 4 + 1) * H], raw1[:, j:j + (H - 1) * F + 1:F], id32[:, :])
                op.then_inc(turned, 1)
            pe.wait_ge(dense_in, 16 * len(DR))
            for m, ts in enumerate(DENSE_TURNS):
                turn = 1 + len(W1_TURNS) + m
                pe.wait_ge(kept_act, turn - 3)
                for c, t in enumerate(ts):
                    op = pe.transpose(turn_bank[turn % 3][0:KD, c // 4, (c % 4) * TB:(c % 4 + 1) * TB], dense[:, t, :], id32[:, :])
                op.then_inc(turned, 1)
            pe.wait_ge(kept_act, len(W1_TURNS))
            pe.wait_ge(kept_dve, 2 + len(DENSE_TURNS))
            turn_embedding(0, 0, 0)
            pe.wait_ge(picks, R * OPS)
            pe.wait_ge(mlp_low, 3)

            def slot(it, q):
                PB = PAIR * BLOCKS

                def choose(k, e):
                    n = ENTRIES * k + e
                    if k % BLOCKS == 0 and e == 0:
                        wait(pe, embT_act, count(it, PAIR, k // BLOCKS + 1))
                        wait(pe, embT_dve, count(it, PAIR, k // BLOCKS + 1))
                    wait(pe, lo_ready, count(it, ENTRIES * PB, n - 1))
                    b0 = (k % BLOCKS) * BB
                    cols = embT[0:KP, (k // BLOCKS) % 2, b0:b0 + BB, :].rearrange("p b d -> p (b d)")
                    for a in range(2) if e == 0 else (1,):
                        op = pe.matmul(ring[e % 2][:, a, :], pick[:, e + a, :], cols, start=True, stop=True)
                    op.then_inc(picked, 1)

                def convolve(k, e):
                    n = ENTRIES * k + e
                    if e == 0:
                        wait(pe, x1_ready, count(it, PB, k))
                    chunks = [(a, 2 * e + a - 1) for a in range(2) if 2 * e + a]
                    wait(pe, hi_ready, count(it, ENTRIES * PB, n + 1))
                    for a, c in chunks:
                        pe.matmul(px[:, :], w0h[0:KP, c, :], hi[0:KP, e, a, :], start=(c == 0), stop=False)
                        pe.matmul(px[:, :], w0l[0:KP, c, :], hi[0:KP, e, a, :], start=False, stop=False)
                    wait(pe, lo_ready, count(it, ENTRIES * PB, n + 1))
                    for a, c in chunks:
                        op = pe.matmul(px[:, :], w0h[0:KP, c, :], lo[0:KP, e, a, :], start=False, stop=(c == CH - 1))
                    op.then_inc(layer0, 1)

                def correlate(kg, half):
                    for a in range(2):
                        g = 2 * half + a
                        terms = ((xTh, 0), (xTl, 0), (xTh, 1))
                        for m, (x, part) in enumerate(terms):
                            op = pe.matmul(mid[:, a, 0:GB * J], x[:, kg % 2, g, :], diag[:, kg % 2, g, :, part, :],
                                           start=(m == 0), stop=(m == len(terms) - 1))
                    op.then_inc(gram_done, 1)

                def second(t, j0, j1):
                    if j0 == 0:
                        wait(pe, gram_kept, count(it, 2 * PB, 2 * BLOCKS * (t + 1)))
                        if t % 2 == 0:
                            wait(pe, y_ready, count(it, 1, t // 2))
                        elif not tail(it):
                            wait(pe, z1_lo, count(it, PAIR, t))
                    for j in range(j0, j1):
                        op = pe.matmul(bank(it, t % 2)[:, 0:TB], w1T[:, j, :], gram[:, t % 2, j, :], start=(j == 0), stop=(j == F - 1))
                    if j1 == F:
                        op.then_inc(out1_done, 1)

                there, k = stage(it, q, 0)
                last, kl = stage(it, q, 1)
                e0 = 2 * (q % 2)
                el = 2 - e0
                if there:
                    choose(k, e0)
                gb, kg = stage(it, q, 7)
                if q % 2 and gb:
                    wait(pe, gram_kept, count(it, 2 * PB, 2 * kg + 1))
                    correlate(kg, 1)
                    if there:
                        choose(k, e0 + 1)
                    if last:
                        convolve(kl, el)
                else:
                    if last:
                        convolve(kl, el)
                    if there:
                        choose(k, e0 + 1)
                turn, t = ahead(it, q, TURN, TURN_LATE)
                if turn and q % SLOTS == TURN:
                    _, kx = stage(it, q, 4)
                    wait(pe, xTl_ready, count(it, PB, kx + 1))
                    turn_embedding(it, t % 2, t)
                if last:
                    convolve(kl, el + 1)
                ga, kg = stage(it, q, 6)
                if q % 2 == 0 and ga:
                    wait(pe, diag_in[kg % 2], count(it, 16 * GB * PB // 2, 16 * GB * (kg // 2 + 1)))
                    after = 0 if isinstance(it, int) and it * PB + kg + 1 == TILES * BLOCKS else 1
                    wait(pe, xTh_ready, count(it, PB, kg + 1 + after))
                    wait(pe, xTl_ready, count(it, PB, kg + 1 + after))
                    if not after:
                        wait(pe, gram_kept, count(it, 2 * PB, 2 * kg))
                    if turn:
                        wait(pe, embT_act, count(it, PAIR, t + 1))
                        wait(pe, embT_dve, count(it, PAIR, t + 1))
                    correlate(kg, 0)
                done, kx = stage(it, q, 3)
                if turn and q % SLOTS != TURN:
                    wait(pe, gram_kept, count(it, 2 * PB, 2 * kx - 2))
                    turn_embedding(it, t % 2, t)
                if q % 2 and done:
                    if turn:
                        wait(pe, embT_act, count(it, PAIR, t + 1))
                        wait(pe, embT_dve, count(it, PAIR, t + 1))
                    wait(pe, x1_ready, count(it, PB, kx + 1))
                    wait(pe, gram_kept, count(it, 2 * PB, 2 * kx - 2))
                    b0 = (kx % BLOCKS) * BB
                    for g in range(GROUPS):
                        pe.transpose(mid[:, 0, g * H:(g + 1) * H], x1[:, kx % 2, g * P:(g + 1) * P], id32[:, :])
                    for g in range(GROUPS):
                        cols = embT[0:KP, (kx // BLOCKS) % 2, b0 + g * GB:b0 + (g + 1) * GB, :].rearrange("p b d -> p (b d)")
                        op = pe.matmul(mid[:, 1, g * J:g * J + F], cols, match[:, 0:F], start=True, stop=True)
                    op.then_inc(x1_turned, 1)

                for lag, n, j0, j1 in TAIL_OUT1 if tail(it) else OUT1:
                    there, s = stage(it, q, lag, S_IT)
                    if q == lag % S_IT and there:
                        second(PAIR * s + n, j0, j1)
                for half in range(2):
                    there, s = stage(it, q, L1_LAG + half, S_IT)
                    if q == (L1_LAG + half) % S_IT and there:
                        if half == 0:
                            wait(pe, out0_lo, count(it, PAIR, PAIR * s + PAIR))
                            wait(pe, z1_lo, count(it, PAIR, PAIR * s + PAIR))
                        elif bank(it, half) is acc:
                            wait(pe, h1_lo, count(it, 2, 2 * s + 1))
                        at = slice((it + s) * ROWS2, (it + s + 1) * ROWS2) if isinstance(it, int) else \
                            bass.ds(it * ROWS2 + s * ROWS2, ROWS2)
                        for a in range(2):
                            w = slice((2 * half + a) * P, (2 * half + a + 1) * P)
                            o = bank(it, half)[:, a * ROWS2:(a + 1) * ROWS2]
                            for c, (xh, xl) in enumerate(((o0h, o0l), (z1h, z1l))):
                                for m, (wt, x) in enumerate(((wt1h, xh), (wt1l, xh), (wt1h, xl))):
                                    pe.matmul(o, wt[:, c, w], x[:, :, :].rearrange("p n b -> p (n b)"), start=(c + m == 0), stop=False)
                            op = pe.matmul(o, wt1d[:, w], denseT[:, at], start=False, stop=True)
                        op.then_inc(l1_done, 1)
                there, s = stage(it, q, L2_LAG, S_IT)
                if q == L2_LAG % S_IT and there:
                    for m in range(N2 // P):
                        w = slice(m * P, (m + 1) * P)
                        for c in range(N1 // P):
                            if m == 0 and c in (0, 2):
                                both = c == 2 or bank(it, 1) is acc
                                wait(pe, h1_lo, count(it, 2, 2 * s + 1 + both))
                            for n, (wt, x) in enumerate(((wt2h, h1h), (wt2l, h1h), (wt2h, h1l))):
                                op = pe.matmul(acc[:, m * ROWS2:(m + 1) * ROWS2], wt[:, c, w], x[:, c, :],
                                               start=(c + n == 0), stop=(c == N1 // P - 1 and n == 2))
                    op.then_inc(l2_done, 1)
                there, s = stage(it, q, L3_LAG, S_IT)
                if q == L3_LAG % S_IT and there:
                    wait(pe, h2_ready, count(it, 1, s + 1))
                    for c in range(N2 // P):
                        op = pe.matmul(acc[0:1, 0:ROWS2], wt3[:, c:c + 1], h2[:, c, :], start=(c == 0), stop=(c == N2 // P - 1))
                    op.then_inc(l3_done, 1)

            slots(pe, slot)


def kernel(**inputs):
    import numpy as _np
    import concourse.bacc as _bacc
    from concourse.bass_utils import run_bass_kernel_spmd as _run

    nc = _bacc.Bacc("TRN2", target_bir_lowering=False, num_devices=1)
    arrays, dram = {}, {}
    names = ["dense_ctx", "ids"] + TABLES + ["W_top1", "b_top1", "W_top2", "b_top2", "W_top3", "L0_rec_W0", "L0_rec_W1"]
    for name in names:
        a = _np.ascontiguousarray(inputs[name])
        arrays[f"in_{name}"] = a
        dram[name] = nc.dram_tensor(f"in_{name}", a.shape, mybir.dt.from_np(a.dtype), kind="ExternalInput").ap()
    y = nc.dram_tensor("out_y", (B, 1), F32, kind="ExternalOutput").ap()
    build(nc, dram["dense_ctx"], dram["ids"], [dram[n] for n in TABLES], dram["W_top1"], dram["b_top1"],
          dram["W_top2"], dram["b_top2"], dram["W_top3"], dram["L0_rec_W0"], dram["L0_rec_W1"], y)
    r = _run(nc, [arrays], core_ids=[0])
    return r.results[0]["out_y"]
```
